# Optimizing a Trainium2 kernel written in Bass

```python
import numpy as np
import jax
import jax.numpy as jnp

def _softmax(x, axis=-1):
    return jax.nn.softmax(x, axis=axis)

def _gelu(x):
    return jax.nn.gelu(x, approximate=True)

def _silu(x):
    return jax.nn.silu(x)

def _sigmoid(x):
    return jax.nn.sigmoid(x)

def _layernorm(x, axis=-1, eps=1e-05):
    m = jnp.mean(x, axis=axis, keepdims=True)
    v = jnp.var(x, axis=axis, keepdims=True)
    return (x - m) / jnp.sqrt(v + eps)

def _scatter_add(tgt, idx, src, axis=0):
    return tgt.at[idx].add(src)

def _segment_sum(src, seg, n):
    return jax.ops.segment_sum(src, seg, n)
kernel_name = 'mk_gnn_resnorm_d2_gnn_r8_e66134'

def setup_inputs(seed: int=0):
    np.random.seed(seed)
    _w = jnp.asarray

    def _rec_inputs():
        import jax
        import jax.numpy as jnp
        _gk = jax.random.key(seed)
        x = -0.0002117 + 1 * jax.random.normal(jax.random.fold_in(_gk, 1), (12500, 256), jnp.float32)
        _s = jax.random.randint(jax.random.fold_in(_gk, 2), (100000,), 0, 12500, jnp.int32)
        _d = jax.random.randint(jax.random.fold_in(_gk, 3), (100000,), 0, 12500, jnp.int32)
        _loop = jnp.arange(12500, dtype=jnp.int32)
        src = jnp.concatenate([_s, _d, _loop])
        dst = jnp.concatenate([_d, _s, _loop])
        _o = jnp.argsort(dst, stable=True)
        src = src[_o]
        dst = dst[_o]
        edge_weight = jax.random.uniform(jax.random.fold_in(_gk, 13), (212500,), jnp.float32, 0.0, 0.999994)
        return (x, src, dst, edge_weight)
    x, src, dst, edge_weight = _rec_inputs()

    def _L0_gnn_setup():
        import jax, jax.numpy as jnp
        import numpy as np
        N = 12500
        E = 200000
        H, F_IN, F_OUT = (8, 256, 32)
        key = jax.random.key(seed)
        k1, k2, k3, k4, k5 = jax.random.split(key, 5)
        x = jax.random.normal(k1, (N, F_IN), dtype=jnp.float32)
        edge_index = jax.random.randint(k2, (2, E), 0, N, dtype=jnp.int64)
        W = jax.random.normal(k3, (H, F_IN, F_OUT), dtype=jnp.float32) * (1.0 / np.sqrt(F_IN))
        a_src = jax.random.normal(k4, (H, F_OUT, 1), dtype=jnp.float32) * 0.1
        a_dst = jax.random.normal(k5, (H, F_OUT, 1), dtype=jnp.float32) * 0.1
        return {'x': x, 'edge_index': edge_index, 'W': W, 'a_src': a_src, 'a_dst': a_dst}
    _L0_gnn_all = _L0_gnn_setup()
    _L0_gnn_in = {k: v for k, v in _L0_gnn_all.items() if k in ('W', 'a_src', 'a_dst')}
    del _L0_gnn_all

    def _L1_gnn_setup():
        import jax, jax.numpy as jnp
        import numpy as np
        NEG_SLOPE = 0.01

        def _leaky(x):
            return jnp.where(x >= 0, x, NEG_SLOPE * x)

        def _gcn(x, W, b, src, dst, w, n):
            h = x @ W
            agg = jax.ops.segment_sum(w[:, None] * h[src], dst, num_segments=n)
            return agg + b
        key = jax.random.key(seed)
        ks = jax.random.split(key, 10)
        N, E, IN, HID, OUT, B = (12500, 37500, 256, 256, 256, 128)
        features = jax.random.normal(ks[0], (N, IN), dtype=jnp.float32)
        values = jax.random.uniform(ks[1], (E,), dtype=jnp.float32)
        s = 1.0 / np.sqrt(IN)
        W1 = jax.random.normal(ks[2], (IN, HID), dtype=jnp.float32) * s
        b1 = jnp.zeros((HID,), dtype=jnp.float32)
        W2 = jax.random.normal(ks[3], (HID + IN, OUT), dtype=jnp.float32) * (1.0 / np.sqrt(HID + IN))
        b2 = jnp.zeros((OUT,), dtype=jnp.float32)
        Wl = jax.random.normal(ks[4], (HID + OUT, IN), dtype=jnp.float32) * (1.0 / np.sqrt(HID + OUT))
        bl = jnp.zeros((IN,), dtype=jnp.float32)
        adjs = jax.random.randint(ks[5], (2, E), 0, N, dtype=jnp.int64)
        batch = jnp.sort(jax.random.randint(ks[6], (N,), 0, B, dtype=jnp.int64))
        root_idx = jax.random.randint(ks[7], (B,), 0, N, dtype=jnp.int64)
        return {'features': features, 'values': values, 'W1': W1, 'b1': b1, 'W2': W2, 'b2': b2, 'Wl': Wl, 'bl': bl, 'adjs': adjs, 'batch': batch, 'root_idx': root_idx}
    _L1_gnn_all = _L1_gnn_setup()
    _L1_gnn_in = {k: v for k, v in _L1_gnn_all.items() if k in ('W1', 'b1', 'W2', 'b2', 'Wl', 'bl', 'root_idx')}
    del _L1_gnn_all
    return {'x': x, 'src': src, 'dst': dst, 'edge_weight': edge_weight, 'L0_gnn_W': _L0_gnn_in['W'], 'L0_gnn_a_src': _L0_gnn_in['a_src'], 'L0_gnn_a_dst': _L0_gnn_in['a_dst'], 'L1_gnn_W1': _L1_gnn_in['W1'], 'L1_gnn_b1': _L1_gnn_in['b1'], 'L1_gnn_W2': _L1_gnn_in['W2'], 'L1_gnn_b2': _L1_gnn_in['b2'], 'L1_gnn_Wl': _L1_gnn_in['Wl'], 'L1_gnn_bl': _L1_gnn_in['bl'], 'L1_gnn_root_idx': _L1_gnn_in['root_idx']}

def reference(x, src, dst, edge_weight, L0_gnn_W, L0_gnn_a_src, L0_gnn_a_dst, L1_gnn_W1, L1_gnn_b1, L1_gnn_W2, L1_gnn_b2, L1_gnn_Wl, L1_gnn_bl, L1_gnn_root_idx):
    import jax
    import jax.numpy as jnp

    def _L0_gnn_ref(x, edge_index, W, a_src, a_dst):
        import jax, jax.numpy as jnp
        import numpy as np
        N = 12500
        E = 200000
        H, F_IN, F_OUT = (8, 256, 32)
        src, dst = (edge_index[0], edge_index[1])
        h = jnp.einsum('ni,hio->hno', x, W)
        attn_src = jnp.einsum('hno,ho->hn', h, a_src[..., 0])
        attn_dst = jnp.einsum('hno,ho->hn', h, a_dst[..., 0])
        edge_attn = jax.nn.leaky_relu(attn_src[:, src] + attn_dst[:, dst], negative_slope=0.2)
        edge_attn_exp = jnp.exp(edge_attn - jnp.max(edge_attn))
        attn_sum = jax.ops.segment_sum(edge_attn_exp.T, dst, num_segments=N)
        attn_norm = edge_attn_exp / (attn_sum[dst].T + 1e-10)
        weighted_h = attn_norm[..., None] * h[:, src]
        out = jax.ops.segment_sum(weighted_h.transpose(1, 0, 2), dst, num_segments=N)
        out = out.reshape(N, H * F_OUT)
        return out + x

    def _L1_gnn_ref(features, values, W1, b1, W2, b2, Wl, bl, adjs, batch, root_idx):
        import jax, jax.numpy as jnp
        import numpy as np
        NEG_SLOPE = 0.01

        def _leaky(x):
            return jnp.where(x >= 0, x, NEG_SLOPE * x)

        def _gcn(x, W, b, src, dst, w, n):
            h = x @ W
            agg = jax.ops.segment_sum(w[:, None] * h[src], dst, num_segments=n)
            return agg + b
        N = features.shape[0]
        src, dst = (adjs[0], adjs[1])
        f1 = features
        h = _gcn(f1, W1, b1, src, dst, values, N)
        f2 = h
        root1 = f1[root_idx[batch]]
        x = _leaky(jnp.concatenate([h, root1], axis=1))
        x = _gcn(x, W2, b2, src, dst, values, N)
        x = _leaky(x)
        root2 = f2[root_idx[batch]]
        x = jnp.concatenate([x, root2], axis=1)
        return _leaky(x @ Wl + bl)
    edge_index = jnp.stack([src, dst])
    batch0 = jnp.zeros((12500,), jnp.int32)
    x = _layernorm(x + _L0_gnn_ref(x, edge_index, L0_gnn_W, L0_gnn_a_src, L0_gnn_a_dst), axis=-1)
    x = _layernorm(x + _L1_gnn_ref(x, edge_weight, L1_gnn_W1, L1_gnn_b1, L1_gnn_W2, L1_gnn_b2, L1_gnn_Wl, L1_gnn_bl, edge_index, batch0, L1_gnn_root_idx), axis=-1)
    return x

_drawn_inputs = setup_inputs


def setup_inputs(seed=0):
    import zlib

    import numpy as np

    out = dict(_drawn_inputs(seed))
    spreads = {'L1_gnn_b1': (0.0, 0.1), 'L1_gnn_b2': (0.0, 0.679), 'L1_gnn_bl': (0.0, 0.313)}
    factors = {'L0_gnn_a_dst': 3.506}
    for name, (base, spread) in spreads.items():
        noise = np.random.default_rng([zlib.crc32(name.encode()), seed]).standard_normal(out[name].shape)
        drawn = base * np.exp(spread * noise) if base else spread * noise
        out[name] = jnp.asarray(drawn.astype(out[name].dtype))
    for name, factor in factors.items():
        out[name] = (out[name] * factor).astype(out[name].dtype)
    return out
```

```python
from collections import namedtuple
from contextlib import ExitStack

import numpy as np
import concourse.bass as bass
from concourse import mybir

F32, I32 = mybir.dt.float32, mybir.dt.int32
ALU = mybir.AluOpType
ACT = mybir.ActivationFunctionType
AX_X = mybir.AxisListType.X

P = 128
GROUP = 4
WINDOW = 64
BLOCK_GROUPS = 3
BLOCK = GROUP * BLOCK_GROUPS
EPS = 1e-5
LOWEST = -3.0e38

Block = namedtuple("Block", "b slot turn group chunk sizes rows")


def at_least(eng, sem, value):
    if isinstance(value, int) and value <= 0:
        return
    eng.wait_ge(sem, value)


def build(nc, a, out):
    x, src, dst, edge_weight = a["x"], a["src"], a["dst"], a["edge_weight"]
    N, D = x.shape
    E = src.shape[0]
    H, _, HD = a["L0_gnn_W"].shape
    KB = D // P
    TW = D + 2 * H
    CHUNKS = -(-E // P)
    LAST_EDGES = E - (CHUNKS - 1) * P
    GROUPS = -(-CHUNKS // GROUP)
    ROWT = -(-CHUNKS // P)
    CPAD = ROWT * P
    FULL_TILES, LAST_NODES = N // P, N % P
    assert D == 2 * P and CHUNKS % GROUP == 1 and LAST_EDGES < P and FULL_TILES % 2 == 1 and LAST_NODES

    TURNS = (CHUNKS - 1) // BLOCK // 2
    TAIL = []
    c, b = TURNS * 2 * BLOCK, TURNS * 2
    while c < CHUNKS:
        full = min(BLOCK, (CHUNKS - 1 - c) // GROUP * GROUP)
        sizes = (GROUP,) * (full // GROUP) if full else (1,)
        TAIL.append(Block(b, b % 2, b // 2, c // GROUP, c, sizes, P if full else LAST_EDGES))
        assert b % 2 == 0 or TAIL[0].sizes == (GROUP,) * len(TAIL[0].sizes)
        c, b = c + sum(sizes), b + 1
    NBLOCKS = b
    assert all(t.group % 2 == t.slot for t in TAIL) and len(TAIL) <= 2

    def full_block(turn, slot):
        b = turn * 2 + slot
        return Block(b, slot, turn, b * BLOCK_GROUPS, b * BLOCK, (GROUP,) * BLOCK_GROUPS, P)

    def over_blocks(eng, step):
        for slot in (0, 1):
            step(full_block(0, slot))
        with eng.Fori(1, TURNS) as turn:
            for slot in (0, 1):
                step(full_block(turn, slot))
        for blk in TAIL:
            step(blk)

    Tile = namedtuple("Tile", "t slot turn n0 rows")

    def over_tile_pairs(eng, *steps):
        def pair(turn, rows):
            for step in steps:
                for slot in (0, 1):
                    t = turn * 2 + slot
                    step(Tile(t, slot, turn, t * P, rows[slot]))
        pair(0, (P, P))
        with eng.Fori(1, FULL_TILES // 2) as turn:
            pair(turn, (P, P))
        pair(FULL_TILES // 2, (P, LAST_NODES))

    TILES = FULL_TILES + 1
    TILE_TURNS = TILES // 2

    with ExitStack() as ctx:
        def sb(name, shape, dt=F32):
            return ctx.enter_context(nc.sbuf_tensor(name, shape, dt))

        def sem(name):
            return ctx.enter_context(nc.semaphore(name))

        def dram(name, shape, dt=F32):
            return nc.dram_tensor(name, shape, dt, kind="Internal").ap()

        table1 = dram("table1", (N, TW))
        table2 = dram("table2", (N, D))
        table3 = dram("table3", (N, D))
        w_cols = dram("w_cols", (P, CPAD))

        sums = sb("sums", [P, KB * N])
        heads = sb("heads", [P, N])
        work = sb("work", [P, 2 * BLOCK * TW])
        idx_cols = sb("idx_cols", [P, CPAD + BLOCK], I32)
        rel_cols = sb("rel_cols", [P, CPAD])
        hot = [sb(f"hot{s}", [P, BLOCK * WINDOW]) for s in (0, 1)]
        hotT = [sb(f"hotT{s}", [WINDOW, GROUP * P]) for s in (0, 1)]
        base_i = sb("base_i", [1, GROUPS], I32)
        idx = [sb(f"idx{s}", [P, BLOCK], I32) for s in (0, 1)]
        adst = [sb(f"adst{s}", [WINDOW, BLOCK_GROUPS * H]) for s in (0, 1)]
        score = sb("score", [P, BLOCK * H])
        leaky = sb("leaky", [P, BLOCK * H])
        prob = [sb(f"prob{s}", [P, BLOCK * H]) for s in (0, 1)]
        top = sb("top", [P, 1])
        run_max = [sb(f"run_max{s}", [1, 1]) for s in (0, 1)]
        neg_max = [sb(f"neg_max{s}", [P, 1]) for s in (0, 1)]
        shrink = [sb(f"shrink{s}", [P, 1]) for s in (0, 1)]
        pos_max = sb("pos_max", [P, 1])
        block_max = sb("block_max", [1, 1])
        ident = sb("ident", [P, P])
        iota_f = sb("iota_f", [P, WINDOW])
        ones = sb("ones", [1, P])
        zero_win = sb("zero_win", [P, WINDOW])
        eps_col = sb("eps_col", [P, 1])
        bias_cols = sb("bias_cols", [P, 2 * KB])
        root_i = sb("root_i", [1, 1], I32)
        root_cols = sb("root_cols", [P, 3 * KB])
        small = [sb(f"small{s}", [P, 32]) for s in (0, 1)]

        REC = 32
        sums3 = sums[:, :].rearrange("p (k n) -> p k n", k=KB)
        idx_view = idx_cols[:, :]

        banks = [ctx.enter_context(nc.psum_tensor(f"bank{i}", [P, 512], F32)) for i in range(8)]

        def gathered(slot, width):
            return work[:, slot * BLOCK * TW:slot * BLOCK * TW + BLOCK * width].rearrange("p (c f) -> p c f", c=BLOCK)

        def carve(region):
            at = [0]

            def take(width):
                at[0] += width
                assert at[0] <= region.shape[1]
                return region[:, at[0] - width:at[0]]
            return take

        take = carve(sums)
        src_rows, dst_rows = take(CPAD).bitcast(I32), take(CPAD).bitcast(I32)
        w_rows = take(CPAD)
        src_f, dst_f, w_stage = take(CPAD), take(CPAD), take(CPAD)
        base_raw = take(GROUPS).bitcast(I32)
        base_f = take(ROWT * P // GROUP)
        base_all = take(ROWT * P // GROUP)
        a_all = take(2 * D)
        a_prod = take(KB * D)
        take = carve(work)
        w0 = take(KB * TW).rearrange("p (k f) -> p k f", k=KB)
        x_in = [take(D) for s in (0, 1)]
        x_t = [take(D).rearrange("p (k n) -> p k n", k=KB) for s in (0, 1)]
        row0 = [take(TW) for s in (0, 1)]
        take = carve(work)
        sums_tile = [take(D).rearrange("p (k n) -> p k n", k=KB) for s in (0, 1)]
        heads_tile = [take(P) for s in (0, 1)]
        x_res = [take(D) for s in (0, 1)]
        att = [take(D) for s in (0, 1)]
        row1 = [take(D) for s in (0, 1)]
        norm1 = [take(D) for s in (0, 1)]
        take = carve(heads)
        w_now = take(CPAD)
        W1s, W2a, W2b, Wla, Wlb = (take(KB * D).rearrange("p (k f) -> p k f", k=KB) for _ in range(5))
        root1_row, root2_row = take(D), take(D)
        root_wide = take(KB * P).rearrange("p (k n) -> p k n", k=KB)
        bl_row = take(D)
        h_t = [take(D).rearrange("p (k n) -> p k n", k=KB) for s in (0, 1)]
        h_pre = [take(D).rearrange("p (k n) -> p k n", k=KB) for s in (0, 1)]
        row2 = [take(D) for s in (0, 1)]
        pre = [take(D) for s in (0, 1)]
        act3 = [take(D) for s in (0, 1)]
        x1_in = [take(D) for s in (0, 1)]
        res3 = [take(D) for s in (0, 1)]
        out3 = [take(D) for s in (0, 1)]

        ident_zero, ident_ok = sem("ident_zero"), sem("ident_ok")
        consts_ok = sem("consts_ok")
        rows_in, rows_zero = sem("rows_in"), sem("rows_zero")
        base_ok, base_mm, base_done = sem("base_ok"), sem("base_mm"), sem("base_done")
        rows_f = sem("rows_f")
        cols_turned, cols_done = sem("cols_turned"), sem("cols_done")
        w_saved = sem("w_saved")
        w0_in, a_in, w0_step, w0_ok = sem("w0_in"), sem("a_in"), sem("w0_step"), sem("w0_ok")
        heads_zero, sums_zero = sem("heads_zero"), sem("sums_zero")

        block = ctx.enter_context(nc.Block())

        waited = sem("waited")

        p0_in = [sem(f"p0_in{s}") for s in (0, 1)]
        p0_turned, p0_copied, p0_mm, p0_row = sem("p0_turned"), sem("p0_copied"), sem("p0_mm"), sem("p0_row")
        p0_out = [sem(f"p0_out{s}") for s in (0, 1)]
        R = []
        for r in range(3):
            R.append({n: sem(f"r{r}_{n}") for n in ("idx_ready", "hot_ready", "added", "group_done")})
            R[r]["rows"] = [sem(f"r{r}_rows{s}") for s in (0, 1)]
        adst_in = [sem(f"adst_in{s}") for s in (0, 1)]
        hotT_turned, hotT_copied, adst_done = sem("hotT_turned"), sem("hotT_copied"), sem("adst_done")
        adst_group = sem("adst_group")
        soft, top_done, top_turned, max_run, max_wide = sem("soft"), sem("top_done"), sem("top_turned"), sem("max_run"), sem("max_wide")
        block_max_done, hot_step = sem("block_max_done"), sem("hot_step")
        neg_ready, prob_ready, scaled = sem("neg_ready"), sem("prob_ready"), sem("scaled")
        p1_x = [sem(f"p1_x{s}") for s in (0, 1)]
        p1_copied, p1_turned, p1_chain, p1_row = sem("p1_copied"), sem("p1_turned"), sem("p1_chain"), sem("p1_row")
        p1_var, p1_dev, p3_var, p3_dev = sem("p1_var"), sem("p1_dev"), sem("p3_var"), sem("p3_dev")
        pos_ready, p1_att = sem("pos_ready"), sem("p1_att")
        p1_out = [sem(f"p1_out{s}") for s in (0, 1)]
        weights_in, root_in, root_x = sem("weights_in"), sem("root_in"), sem("root_x")
        root_step, root_mm, root_ok = sem("root_step"), sem("root_mm"), sem("root_ok")
        zero2, zero3 = sem("zero2"), sem("zero3")
        p2_h, p2_act, p2_z, p2_row = sem("p2_h"), sem("p2_act"), sem("p2_z"), sem("p2_row")
        p2_out = [sem(f"p2_out{s}") for s in (0, 1)]
        p2_leaky, p3_in = sem("p2_leaky"), sem("p3_in")
        root2_mm, root2_step, root2_ok = sem("root2_mm"), sem("root2_step"), sem("root2_ok")
        p3_act, p3_mm, p3_pre, p3_leaky, p3_chain, p3_row = (sem("p3_act"), sem("p3_mm"), sem("p3_pre"), sem("p3_leaky"),
                                                             sem("p3_chain"), sem("p3_row"))
        p3_x = [sem(f"p3_x{s}") for s in (0, 1)]
        p3_out = [sem(f"p3_out{s}") for s in (0, 1)]

        tables = [table1, table2, table3]
        widths = [TW, D, D]
        FT = (CHUNKS - 1) // P
        part = CHUNKS - 1 - FT * P
        N_ROW_DMAS = 3 * 3 + 2

        @block.sync
        def _(sp):
            sp.wait_ge(rows_zero, 3)
            for rows, flat in ((dst_rows, dst), (src_rows, src), (w_rows, edge_weight)):
                r3 = rows.rearrange("p (k e) -> p k e", k=ROWT)
                if FT:
                    sp.dma_start(r3[:, 0:FT, :], flat[0:FT * P * P].rearrange("(k p e) -> p k e", p=P, e=P)).then_inc(rows_in, 16)
                sp.dma_start(r3[0:part, FT, :], flat[FT * P * P:(CHUNKS - 1) * P].rearrange("(p e) -> p e", e=P)).then_inc(rows_in, 16)
                sp.dma_start(r3[part:part + 1, FT, 0:LAST_EDGES],
                             flat[(CHUNKS - 1) * P:E].rearrange("(p e) -> p e", p=1)).then_inc(rows_in, 16)
            span = GROUP * P
            sp.dma_start(base_raw[0:1, 0:GROUPS - 1],
                         dst[0:(GROUPS - 1) * span].rearrange("(o g e) -> o g e", o=1, e=span)[:, :, 0],
                         allow_slow_non_contiguous=True).then_inc(rows_in, 16)
            sp.dma_start(base_raw[0:1, GROUPS - 1:GROUPS],
                         dst[(GROUPS - 1) * span:(GROUPS - 1) * span + 1].rearrange("(o g) -> o g", o=1)).then_inc(rows_in, 16)

            def load_x(tile):
                at_least(sp, p0_turned, tile.t - 1)
                sp.dma_start(x_in[tile.slot][0:tile.rows, :], x[bass.ds(tile.n0, tile.rows), :]).then_inc(p0_in[tile.slot], 16)
            over_tile_pairs(sp, load_x)
            sp.wait_ge(cols_done, 3 * ROWT)
            sp.dma_start(w_cols, w_stage).then_inc(w_saved, 16)

            for s in (0, 1):
                sp.wait_ge(p0_out[s], 16 * TILE_TURNS)

            def load_adst(blk):
                at_least(sp, adst_done, blk.b - 1)
                for q in range(len(blk.sizes)):
                    base = sp.value_load(base_i[0:1, bass.ds(blk.group + q, 1)], min_val=0, max_val=N - WINDOW)
                    sp.dma_start(adst[blk.slot][:, q * H:(q + 1) * H],
                                 table1[bass.ds(base, WINDOW), D + H:TW]).then_inc(adst_in[blk.slot], 16)
            over_blocks(sp, load_adst)

            sp.wait_ge(R[0]["added"], GROUPS)

            def load_res(tile):
                at_least(sp, p1_row, tile.t - 1)
                sp.dma_start(x_res[tile.slot][0:tile.rows, :], x[bass.ds(tile.n0, tile.rows), :]).then_inc(p1_x[tile.slot], 16)
            over_tile_pairs(sp, load_res)
            sp.wait_ge(p1_turned, TILES)
            sp.wait_ge(p1_copied, 2 * TILES)
            sp.dma_start(w_now, w_cols).then_inc(weights_in, 16)
            for tile, w in ((W1s, a["L1_gnn_W1"]), (W2a, a["L1_gnn_W2"][0:D, :]), (W2b, a["L1_gnn_W2"][D:2 * D, :]),
                            (Wla, a["L1_gnn_Wl"][0:D, :]), (Wlb, a["L1_gnn_Wl"][D:2 * D, :])):
                sp.dma_start(tile, w.rearrange("(k p) f -> p k f", p=P)).then_inc(weights_in, 16)
            sp.dma_start(bl_row[0:1, :], a["L1_gnn_bl"].rearrange("(o f) -> o f", o=1)).then_inc(weights_in, 16)
            sp.dma_start(bias_cols[:, 0:KB], a["L1_gnn_b1"].rearrange("(k p) -> p k", p=P),
                         allow_slow_non_contiguous=True).then_inc(weights_in, 16)
            sp.dma_start(bias_cols[:, KB:2 * KB], a["L1_gnn_b2"].rearrange("(k p) -> p k", p=P),
                         allow_slow_non_contiguous=True).then_inc(weights_in, 16)
            sp.dma_start(root_i[:, :], a["L1_gnn_root_idx"][0:1].rearrange("(o f) -> o f", o=1)).then_inc(root_in, 16)
            sp.wait_ge(root_in, 16)
            for s in (0, 1):
                sp.wait_ge(p1_out[s], 16 * TILE_TURNS)
            root = sp.value_load(root_i[0:1, 0:1], min_val=0, max_val=N - 1)
            sp.dma_start(root_cols[:, 0:KB], table2[bass.ds(root, 1), :].rearrange("o (k p) -> p (o k)", p=P),
                         allow_slow_non_contiguous=True).then_inc(root_x, 16)

            sp.wait_ge(R[2]["added"], GROUPS)

            def load_x1(tile):
                at_least(sp, p3_row, tile.t - 1)
                sp.dma_start(x1_in[tile.slot][0:tile.rows, :], table2[bass.ds(tile.n0, tile.rows), :]).then_inc(p3_x[tile.slot], 16)
            over_tile_pairs(sp, load_x1)
            for s in (0, 1):
                sp.wait_ge(p3_out[s], 16 * TILE_TURNS)

        @block.gpsimd
        def _(pool):
            pool.memset(ident[:, :], 0.0).then_inc(ident_zero, 1)
            pool.wait_ge(ident_zero, 1)
            pool.affine_select(out=ident[:, :], in_=ident[:, :], compare_op=ALU.not_equal, fill=1.0, base=0,
                               pattern=[[-1, P]], channel_multiplier=1).then_inc(ident_ok, 1)
            pool.iota(iota_f[:, :], pattern=[[1, WINDOW]], base=0, channel_multiplier=0,
                      allow_small_or_imprecise_dtypes=True).then_inc(consts_ok, 1)
            pool.memset(ones[:, :], 1.0).then_inc(consts_ok, 1)
            pool.memset(zero_win[:, :], 0.0).then_inc(consts_ok, 1)
            pool.memset(eps_col[:, :], EPS).then_inc(consts_ok, 1)
            pool.memset(neg_max[1][:, :], -LOWEST).then_inc(consts_ok, 1)
            pool.memset(run_max[1][:, :], LOWEST).then_inc(consts_ok, 1)
            pool.memset(idx_cols[:, CPAD:CPAD + BLOCK], 0).then_inc(consts_ok, 1)
            pool.memset(heads[:, :], 0.0).then_inc(heads_zero, 1)
            pool.wait_ge(cols_done, 3 * ROWT)
            pool.wait_ge(w_saved, 16)
            pool.wait_ge(w0_ok, 1)
            pool.memset(sums[:, :], 0.0).then_inc(sums_zero, 1)

            def gather(r):
                def step(blk):
                    pool.wait_ge(R[r]["idx_ready"], blk.b + 1)
                    at_least(pool, R[r]["added"], (blk.b - 1) * BLOCK_GROUPS)
                    pool.sem_inc(waited, 1)
                    for c in range(sum(blk.sizes)):
                        pool.indirect_dma_start(
                            gathered(blk.slot, widths[r])[0:blk.rows, c, :], None, tables[r],
                            bass.IndirectOffsetOnAxis(ap=idx[blk.slot][0:blk.rows, c:c + 1], axis=0),
                        ).then_inc(R[r]["rows"][blk.slot], 16)
                over_blocks(pool, step)

            for s in (0, 1):
                pool.wait_ge(p0_out[s], 16 * TILE_TURNS)
            gather(0)
            for s in (0, 1):
                pool.wait_ge(p1_out[s], 16 * TILE_TURNS)
            pool.memset(sums3[:, 1, :], 0.0).then_inc(zero2, 1)
            gather(1)
            for s in (0, 1):
                pool.wait_ge(p2_out[s], 16 * TILE_TURNS)
            pool.wait_ge(root2_ok, 1)
            pool.memset(sums3[:, 1, :], 0.0).then_inc(zero3, 1)
            gather(2)

        @block.scalar
        def _(act):
            for k in range(KB):
                act.dma_start(w0[:, k, 0:D].rearrange("p (h o) -> p h o", h=H),
                              a["L0_gnn_W"][:, k * P:(k + 1) * P, :].rearrange("h p o -> p h o")).then_inc(w0_in, 16)
            for j, name in enumerate(("L0_gnn_a_src", "L0_gnn_a_dst")):
                act.dma_start(a_all[:, j * D:(j + 1) * D],
                              a[name].rearrange("h o u -> (u h o)").partition_broadcast(P)).then_inc(a_in, 16)

            def copy_xt(tile):
                act.wait_ge(p0_turned, tile.t + 1)
                at_least(act, p0_mm, tile.t - 1)
                act.activation(x_t[tile.slot][:, :, 0:tile.rows],
                               banks[tile.slot][:, 0:D].rearrange("p (k n) -> p k n", k=KB)[:, :, 0:tile.rows],
                               ACT.Copy).then_inc(p0_copied, 1)

            def store_row0(tile):
                act.wait_ge(p0_row, tile.t + 1)
                act.dma_start(table1[bass.ds(tile.n0, tile.rows), :], row0[tile.slot][0:tile.rows, :]).then_inc(p0_out[tile.slot], 16)
            over_tile_pairs(act, copy_xt, store_row0)

            def copy_idx(r, slot, chunk):
                act.activation(idx[slot][:, :], idx_cols[:, bass.ds(chunk, BLOCK)], ACT.Copy).then_inc(R[r]["idx_ready"], 1)

            def next_idx(r, blk):
                if blk is TAIL[-1]:
                    return
                at_least(act, R[r]["rows"][1 - blk.slot], 16 * BLOCK * (blk.turn + blk.slot))
                act.sem_inc(waited, 1)
                copy_idx(r, 1 - blk.slot, blk.chunk + sum(blk.sizes))

            act.wait_ge(cols_done, 3 * ROWT)
            act.wait_ge(consts_ok, 7)
            copy_idx(0, 0, 0)

            def softmax(blk):
                n, rows, s = sum(blk.sizes), blk.rows, blk.slot
                next_idx(0, blk)
                for q, size in enumerate(blk.sizes):
                    half = (s + q) % 2
                    act.wait_ge(hotT_turned, blk.group + q + 1)
                    at_least(act, adst_group, blk.group + q - 1)
                    act.sem_inc(waited, 1)
                    act.activation(hotT[half][:, 0:size * P].rearrange("p (c e) -> p c e", e=P)[:, :, 0:rows],
                                   banks[half][0:WINDOW, 0:size * P].rearrange("p (c e) -> p c e", e=P)[:, :, 0:rows],
                                   ACT.Copy).then_inc(hotT_copied, 1)
                act.wait_ge(max_wide, blk.b + 1)
                act.activation(neg_max[s][:, :], banks[5][:, P:P + 1], ACT.Copy, scale=-1.0).then_inc(neg_ready, 1)
                act.wait_ge(neg_ready, blk.b + 1)
                act.activation(shrink[s][:, :], neg_max[1 - s][:, :], ACT.Exp, bias=neg_max[s][:, 0:1], scale=-1.0).then_inc(prob_ready, 1)
                act.activation(prob[s][0:rows, 0:n * H], leaky[0:rows, 0:n * H], ACT.Exp,
                               bias=neg_max[s][0:rows, 0:1]).then_inc(prob_ready, 1)
            over_blocks(act, softmax)

            act.wait_ge(R[0]["added"], GROUPS)
            last = TAIL[-1].slot
            act.activation(pos_max[:, :], neg_max[last][:, :], ACT.Copy, scale=-1.0).then_inc(pos_ready, 1)
            act.wait_ge(pos_ready, 1)
            act.activation(heads[REC:REC + 1, :], heads[REC:REC + 1, :], ACT.Exp, bias=pos_max[REC:REC + 1, 0:1]).then_inc(pos_ready, 1)
            act.wait_ge(pos_ready, 2)

            def copy_tile(tile):
                at_least(act, p1_turned, tile.t - 1)
                act.sem_inc(waited, 1)
                act.activation(sums_tile[tile.slot][:, :, 0:tile.rows], sums3[:, :, bass.ds(tile.n0, tile.rows)],
                               ACT.Copy).then_inc(p1_copied, 1)
                act.activation(heads_tile[tile.slot][0:REC + 1, 0:tile.rows], heads[0:REC + 1, bass.ds(tile.n0, tile.rows)],
                               ACT.Copy).then_inc(p1_copied, 1)

            def root_var(var_ready, done):
                def step(tile):
                    act.wait_ge(var_ready, tile.t + 1)
                    act.activation(small[tile.slot][0:tile.rows, 24:25], small[tile.slot][0:tile.rows, 23:24], ACT.Sqrt,
                                   bias=eps_col[0:tile.rows, 0:1]).then_inc(done, 1)
                return step

            def store_row1(tile):
                act.wait_ge(p1_row, tile.t + 1)
                act.dma_start(table2[bass.ds(tile.n0, tile.rows), :], norm1[tile.slot][0:tile.rows, :]).then_inc(p1_out[tile.slot], 16)
            over_tile_pairs(act, copy_tile, root_var(p1_var, p1_dev), store_row1)
            copy_idx(1, 0, 0)

            act.wait_ge(weights_in, 16 * 9)

            def idx_only(r):
                def step(blk):
                    next_idx(r, blk)
                return step
            over_blocks(act, idx_only(1))

            def act_h(tile):
                act.wait_ge(p2_h, tile.t + 1)
                at_least(act, p2_leaky, tile.t - 1)
                for k in range(KB):
                    act.activation(h_pre[tile.slot][:, k, 0:tile.rows], banks[tile.slot][:, k * P:k * P + tile.rows], ACT.Identity,
                                   bias=bias_cols[:, k:k + 1]).then_inc(p2_act, 1)

            def store_row2(tile):
                act.wait_ge(p2_row, tile.t + 1)
                act.dma_start(table3[bass.ds(tile.n0, tile.rows), :], row2[tile.slot][0:tile.rows, :]).then_inc(p2_out[tile.slot], 16)
            over_tile_pairs(act, act_h, store_row2)
            copy_idx(2, 0, 0)
            over_blocks(act, idx_only(2))

            act.wait_ge(R[2]["added"], GROUPS)

            def act_sums(tile):
                at_least(act, p3_in, tile.t - 1)
                act.sem_inc(waited, 1)
                for k in range(KB):
                    act.activation(h_pre[tile.slot][:, k, 0:tile.rows], sums3[:, k, bass.ds(tile.n0, tile.rows)], ACT.Identity,
                                   bias=bias_cols[:, KB + k:KB + k + 1]).then_inc(p3_act, 1)

            def store_out(tile):
                act.wait_ge(p3_row, tile.t + 1)
                act.dma_start(out[bass.ds(tile.n0, tile.rows), :], out3[tile.slot][0:tile.rows, :]).then_inc(p3_out[tile.slot], 16)
            over_tile_pairs(act, act_sums, root_var(p3_var, p3_dev), store_out)

        @block.tensor
        def _(pe):
            pe.wait_ge(ident_ok, 1)
            pe.wait_ge(consts_ok, 7)
            pe.wait_ge(base_ok, 1)
            pe.matmul(banks[2][:, 0:ROWT * P // GROUP], ones[0:1, :], base_f[0:1, :], start=True, stop=True).then_inc(base_mm, 1)
            pe.wait_ge(rows_f, 2)
            for k in range(ROWT):
                at_least(pe, cols_done, 3 * (k - 1))
                for j, rows in enumerate((dst_f, src_f, w_rows)):
                    pe.transpose(banks[k % 2][:, j * P:(j + 1) * P], rows[:, k * P:(k + 1) * P], ident[:, :]).then_inc(cols_turned, 1)
            pe.wait_ge(cols_done, 3 * ROWT)

            pe.wait_ge(w0_ok, 1)

            def turn_x(tile):
                pe.wait_ge(p0_in[tile.slot], 16 * (tile.turn + 1))
                at_least(pe, p0_copied, tile.t - 1)
                for k in range(KB):
                    mm = pe.transpose(banks[tile.slot][:, k * P:k * P + tile.rows], x_in[tile.slot][0:tile.rows, k * P:(k + 1) * P],
                                      ident[0:tile.rows, 0:tile.rows])
                mm.then_inc(p0_turned, 1)

            def mm_x(tile):
                pe.wait_ge(p0_copied, tile.t + 1)
                at_least(pe, p0_row, tile.t - 1)
                for k in range(KB):
                    mm = pe.matmul(banks[2 + tile.slot][0:tile.rows, 0:TW], x_t[tile.slot][:, k, 0:tile.rows], w0[:, k, :],
                                   start=(k == 0), stop=(k == KB - 1))
                mm.then_inc(p0_mm, 1)
            over_tile_pairs(pe, turn_x, mm_x)

            def windows(blk):
                n, rows, s = sum(blk.sizes), blk.rows, blk.slot
                pe.wait_ge(R[0]["hot_ready"], blk.b + 1)

                def turn(q):
                    half = (s + q) % 2
                    at_least(pe, hotT_copied, blk.group + q - 1)
                    pe.sem_inc(waited, 1)
                    for c in range(blk.sizes[q]):
                        cc = q * GROUP + c
                        mm = pe.transpose(banks[half][0:WINDOW, c * P:c * P + rows], hot[s][0:rows, cc * WINDOW:(cc + 1) * WINDOW],
                                          ident[0:rows, 0:rows])
                    mm.then_inc(hotT_turned, 1)

                def pick(q):
                    half = (s + q) % 2
                    pe.wait_ge(hotT_copied, blk.group + q + 1)
                    for c in range(blk.sizes[q]):
                        cc = q * GROUP + c
                        mm = pe.matmul(banks[4][0:rows, cc * H:(cc + 1) * H], hotT[half][:, c * P:c * P + rows],
                                       adst[s][:, q * H:(q + 1) * H], start=True, stop=True)
                    mm.then_inc(adst_group, 1)
                    return mm
                parts = len(blk.sizes)
                turn(0)
                groups_in_slot = blk.turn * BLOCK_GROUPS + parts
                for q in range(parts):
                    if q + 1 < parts:
                        turn(q + 1)
                    if q == 0:
                        pe.wait_ge(adst_in[s], 16 * groups_in_slot)
                    pick(q)
                pe.wait_ge(adst_group, blk.group + parts)
                pe.sem_inc(adst_done, 1)

            def attend(blk):
                n, rows, s = sum(blk.sizes), blk.rows, blk.slot
                windows(blk)
                pe.wait_ge(top_done, blk.b + 1)
                pe.transpose(banks[5][0:1, 0:rows], top[0:rows, 0:1], ident[0:rows, 0:rows]).then_inc(top_turned, 1)
                pe.wait_ge(max_run, blk.b + 1)
                pe.matmul(banks[5][:, P:P + 1], ones[0:1, :], run_max[s][0:1, 0:1], start=True, stop=True).then_inc(max_wide, 1)
                rowsv = gathered(s, TW)
                for q, size in enumerate(blk.sizes):
                    half = (s + q) % 2
                    pe.wait_ge(scaled, blk.group + q + 1)
                    at_least(pe, R[0]["added"], blk.group + q - 1)
                    for k in range(KB):
                        for c in range(size):
                            cc = q * GROUP + c
                            pe.matmul(banks[2 + half][:, k * WINDOW:(k + 1) * WINDOW], rowsv[0:rows, cc, k * P:(k + 1) * P],
                                      hot[s][0:rows, cc * WINDOW:(cc + 1) * WINDOW], start=(c == 0), stop=(c == size - 1))
                    for c in range(size):
                        cc = q * GROUP + c
                        mm = pe.matmul(banks[6 + half][0:H, 0:WINDOW], prob[s][0:rows, cc * H:(cc + 1) * H],
                                       hot[s][0:rows, cc * WINDOW:(cc + 1) * WINDOW], start=(c == 0), stop=(c == size - 1))
                    mm.then_inc(R[0]["group_done"], 1)
            over_blocks(pe, attend)

            def turn_sums(tile):
                pe.wait_ge(p1_copied, 2 * tile.t + 2)
                at_least(pe, p1_row, tile.t - 1)
                n = tile.rows
                for k in range(KB):
                    pe.transpose(banks[tile.slot][0:n, k * P:(k + 1) * P], sums_tile[tile.slot][:, k, 0:n], ident[:, :])
                pe.transpose(banks[tile.slot][0:n, D:D + REC + 1], heads_tile[tile.slot][0:REC + 1, 0:n],
                             ident[0:REC + 1, 0:REC + 1]).then_inc(p1_turned, 1)
            over_tile_pairs(pe, turn_sums)

            pe.wait_ge(weights_in, 16 * 9)
            pe.wait_ge(root_step, 2)
            for k in range(KB):
                mm = pe.matmul(banks[4][:, 0:D], root_wide[:, k, :], W2b[:, k, :], start=(k == 0), stop=(k == KB - 1))
            mm.then_inc(root_mm, 1)

            def aggregate(r):
                def step(blk):
                    n, rows, s = sum(blk.sizes), blk.rows, blk.slot
                    rowsv = gathered(s, D)
                    pe.wait_ge(R[r]["hot_ready"], blk.b + 1)
                    pe.wait_ge(R[r]["rows"][s], 16 * (blk.turn * BLOCK + n))
                    for q, size in enumerate(blk.sizes):
                        half = (s + q) % 2
                        at_least(pe, R[r]["added"], blk.group + q - 1)
                        for k in range(KB):
                            for c in range(size):
                                cc = q * GROUP + c
                                mm = pe.matmul(banks[2 + half][:, k * WINDOW:(k + 1) * WINDOW], rowsv[0:rows, cc, k * P:(k + 1) * P],
                                               hot[s][0:rows, cc * WINDOW:(cc + 1) * WINDOW], start=(c == 0), stop=(c == size - 1))
                        mm.then_inc(R[r]["group_done"], 1)
                over_blocks(pe, step)
            aggregate(1)

            pe.wait_ge(R[1]["added"], GROUPS)
            pe.wait_ge(root_in, 16)
            root = pe.value_load(root_i[0:1, 0:1], min_val=0, max_val=N - 1)
            for f in range(KB):
                for k in range(KB):
                    mm = pe.matmul(banks[4][:, f:f + 1], W1s[:, k, f * P:(f + 1) * P], sums3[:, k, bass.ds(root, 1)],
                                   start=(k == 0), stop=(k == KB - 1))
            mm.then_inc(root2_mm, 1)
            pe.wait_ge(root2_step, 2)
            for k in range(KB):
                pe.matmul(banks[5][:, 0:D], root_wide[:, k, :], Wlb[:, k, :], start=(k == 0), stop=False)
            pe.matmul(banks[5][:, 0:D], ones[0:1, :], bl_row[0:1, :], start=False, stop=True).then_inc(root2_mm, 1)

            def mm_h(tile):
                at_least(pe, p2_act, 2 * (tile.t - 1))
                for f in range(KB):
                    for k in range(KB):
                        mm = pe.matmul(banks[tile.slot][:, f * P:f * P + tile.rows], W1s[:, k, f * P:(f + 1) * P],
                                       sums3[:, k, bass.ds(tile.n0, tile.rows)], start=(k == 0), stop=(k == KB - 1))
                mm.then_inc(p2_h, 1)

            def mm_z(tile):
                pe.wait_ge(p2_leaky, tile.t + 1)
                at_least(pe, p2_row, tile.t - 1)
                for k in range(KB):
                    mm = pe.matmul(banks[2 + tile.slot][0:tile.rows, 0:D], h_t[tile.slot][:, k, 0:tile.rows], W2a[:, k, :],
                                   start=(k == 0), stop=(k == KB - 1))
                mm.then_inc(p2_z, 1)
            over_tile_pairs(pe, mm_h, mm_z)

            aggregate(2)

            def mm_out(tile):
                pe.wait_ge(p3_in, tile.t + 1)
                at_least(pe, p3_pre, tile.t - 1)
                for k in range(KB):
                    mm = pe.matmul(banks[tile.slot][0:tile.rows, 0:D], h_t[tile.slot][:, k, 0:tile.rows], Wla[:, k, :],
                                   start=(k == 0), stop=(k == KB - 1))
                mm.then_inc(p3_mm, 1)
            over_tile_pairs(pe, mm_out)

        @block.vector
        def _(dve):
            for rows in (dst_rows, src_rows, w_rows):
                dve.memset(rows[:, FT * P:CPAD], 0).then_inc(rows_zero, 1)
            dve.memset(base_f[0:1, :], 0.0).then_inc(base_done, 1)
            dve.wait_ge(w0_in, 16 * KB)
            dve.wait_ge(a_in, 32)
            for j in (0, 1):
                for k in range(KB):
                    dve.tensor_tensor(a_prod[:, k * D:(k + 1) * D], w0[:, k, 0:D], a_all[:, j * D:(j + 1) * D], ALU.mult).then_inc(w0_step, 1)
                dve.wait_ge(w0_step, (j + 1) * KB + j)
                red = dve.tensor_reduce(w0[:, :, D + j * H:D + (j + 1) * H],
                                        a_prod.rearrange("p (k h o) -> p k h o", k=KB, h=H), AX_X, ALU.add)
                if j == 0:
                    red.then_inc(w0_step, 1)
                    dve.wait_ge(w0_step, KB + 1)
                else:
                    red.then_inc(w0_ok, 1)
            dve.wait_ge(rows_in, 16 * N_ROW_DMAS)
            dve.wait_ge(base_done, 1)
            dve.tensor_scalar(base_f[0:1, 0:GROUPS], base_raw[0:1, :], float(N - WINDOW), None, ALU.min).then_inc(base_ok, 1)
            dve.tensor_copy(src_f, src_rows).then_inc(rows_f, 1)
            dve.tensor_copy(dst_f, dst_rows).then_inc(rows_f, 1)
            dve.wait_ge(base_ok, 1)
            dve.tensor_copy(base_i[0:1, :], base_f[0:1, 0:GROUPS]).then_inc(base_done, 1)
            dve.wait_ge(base_mm, 1)
            dve.tensor_copy(base_all, banks[2][:, 0:ROWT * P // GROUP]).then_inc(base_done, 1)
            dve.wait_ge(base_done, 3)
            for k in range(ROWT):
                dve.wait_ge(cols_turned, 3 * k + 3)
                bank = banks[k % 2]
                g = P // GROUP
                dve.tensor_tensor(rel_cols[:, k * P:(k + 1) * P].rearrange("p (g c) -> p g c", c=GROUP),
                                  bank[:, 0:P].rearrange("p (g c) -> p g c", c=GROUP),
                                  base_all[:, k * g:(k + 1) * g].unsqueeze(2).broadcast_to((P, g, GROUP)), ALU.subtract).then_inc(cols_done, 1)
                dve.tensor_copy(idx_cols[:, k * P:(k + 1) * P], bank[:, P:2 * P]).then_inc(cols_done, 1)
                dve.tensor_copy(w_stage[:, k * P:(k + 1) * P], bank[:, 2 * P:3 * P]).then_inc(cols_done, 1)

            def copy_row0(tile):
                dve.wait_ge(p0_mm, tile.t + 1)
                at_least(dve, p0_out[tile.slot], 16 * tile.turn)
                dve.tensor_copy(row0[tile.slot][0:tile.rows, :], banks[2 + tile.slot][0:tile.rows, 0:TW]).then_inc(p0_row, 1)
            over_tile_pairs(dve, copy_row0)

            def one_hot(r, blk, done):
                n, s, rows = sum(blk.sizes), blk.slot, blk.rows
                ins = dve.tensor_tensor(
                    hot[s][0:rows, 0:n * WINDOW].rearrange("p (c j) -> p c j", j=WINDOW),
                    rel_cols[0:rows, bass.ds(blk.chunk, n)].unsqueeze(2).broadcast_to((rows, n, WINDOW)),
                    iota_f[0:rows, :].unsqueeze(1).broadcast_to((rows, n, WINDOW)), ALU.is_equal)
                ins.then_inc(done, 1)

            def window_start(blk, q):
                return dve.value_load(base_i[0:1, bass.ds(blk.group + q, 1)], min_val=0, max_val=N - WINDOW)

            dve.wait_ge(consts_ok, 7)
            dve.wait_ge(sums_zero, 1)
            dve.wait_ge(heads_zero, 1)

            def attend(blk):
                n, rows, s = sum(blk.sizes), blk.rows, blk.slot
                step = blk.b * 2
                rowsv = gathered(s, TW)[0:rows, 0:n, :]
                one_hot(0, blk, R[0]["hot_ready"])
                sc = score[0:rows, 0:n * H].rearrange("p (c h) -> p c h", h=H)
                dve.wait_ge(adst_group, blk.group + len(blk.sizes))
                dve.wait_ge(R[0]["rows"][s], 16 * (blk.turn * BLOCK + n))
                dve.tensor_tensor(sc, rowsv[:, :, D:D + H], banks[4][0:rows, 0:n * H].rearrange("p (c h) -> p c h", h=H),
                                  ALU.add).then_inc(soft, 1)
                dve.wait_ge(soft, step + 1)
                dve.scalar_tensor_tensor(out=leaky[0:rows, 0:n * H], in0=score[0:rows, 0:n * H], scalar=0.2,
                                         in1=score[0:rows, 0:n * H], op0=ALU.mult, op1=ALU.max).then_inc(soft, 1)
                dve.wait_ge(soft, step + 2)
                dve.tensor_reduce(top[0:rows, :], leaky[0:rows, 0:n * H], AX_X, ALU.max).then_inc(top_done, 1)
                dve.wait_ge(top_turned, blk.b + 1)
                dve.tensor_reduce(block_max[0:1, :], banks[5][0:1, 0:rows], AX_X, ALU.max).then_inc(block_max_done, 1)
                dve.wait_ge(block_max_done, blk.b + 1)
                dve.tensor_tensor(run_max[s][:, :], block_max[:, :], run_max[1 - s][:, :], ALU.max).then_inc(max_run, 1)
                dve.wait_ge(prob_ready, blk.b * 2 + 2)
                for q, size in enumerate(blk.sizes):
                    c0 = q * GROUP
                    v = gathered(s, TW)[0:rows, c0:c0 + size, 0:D].rearrange("p c (h o) -> p c h o", h=H)
                    pr = prob[s][0:rows, c0 * H:(c0 + size) * H].rearrange("p (c h) -> p c h", h=H)
                    dve.tensor_tensor(v, v, pr.unsqueeze(3).broadcast_to((rows, size, H, HD)), ALU.mult).then_inc(scaled, 1)
                for q, size in enumerate(blk.sizes):
                    half = (s + q) % 2
                    base = window_start(blk, q)
                    dve.wait_ge(R[0]["group_done"], blk.group + q + 1)
                    at_least(dve, R[0]["added"], blk.group + q)
                    win = sums3[:, :, bass.ds(base, WINDOW)]
                    new = banks[2 + half][:, 0:KB * WINDOW].rearrange("p (k j) -> p k j", k=KB)
                    hwin, hnew = heads[0:H, bass.ds(base, WINDOW)], banks[6 + half][0:H, 0:WINDOW]
                    if q == 0:
                        dve.scalar_tensor_tensor(out=win, in0=win, scalar=shrink[s][:, 0:1], in1=new, op0=ALU.mult, op1=ALU.add)
                        dve.scalar_tensor_tensor(out=hwin, in0=hwin, scalar=shrink[s][0:H, 0:1], in1=hnew, op0=ALU.mult, op1=ALU.add)
                    else:
                        dve.tensor_tensor(win, win, new, ALU.add)
                        dve.tensor_tensor(hwin, hwin, hnew, ALU.add)
                    dve.tensor_scalar(heads[REC:REC + 1, bass.ds(base, WINDOW)], zero_win[REC:REC + 1, :], neg_max[s][REC:REC + 1, 0:1],
                                      None, ALU.add).then_inc(R[0]["added"], 1)
            over_blocks(dve, attend)

            def moments(tile, y, chain, count, done):
                n, s = tile.rows, tile.slot
                dve.wait_ge(chain, count)
                dve.bn_stats(small[s][0:n, 16:22], y).then_inc(chain, 1)
                dve.wait_ge(chain, count + 1)
                dve.sem_inc(waited, 1)
                dve.bn_aggr(small[s][0:n, 22:24], small[s][0:n, 16:22]).then_inc(done, 1)

            def normalize(y, row_out, dev, chain, per, out_sem, done):
                def step(tile):
                    n, s = tile.rows, tile.slot
                    dve.wait_ge(dev, tile.t + 1)
                    dve.reciprocal(small[s][0:n, 25:26], small[s][0:n, 24:25]).then_inc(chain, 1)
                    at_least(dve, out_sem[s], 16 * tile.turn)
                    dve.wait_ge(chain, tile.turn * 2 * per + 2 * (per - 1) + s + 1)
                    dve.tensor_scalar(row_out[s][0:n, :], y[s][0:n, :], small[s][0:n, 22:23], small[s][0:n, 25:26],
                                      ALU.subtract, ALU.mult).then_inc(done, 1)
                return step

            PER1 = 6

            def finish1(tile):
                n, s = tile.rows, tile.slot
                rcp = small[s][0:n, 8:8 + H]
                k = tile.turn * 2 * PER1 + s * (PER1 - 1)
                dve.wait_ge(p1_turned, tile.t + 1)
                dve.tensor_copy(small[s][0:n, 0:1], banks[s][0:n, D + REC:D + REC + 1]).then_inc(p1_chain, 1)
                dve.wait_ge(p1_chain, k + 1)
                dve.scalar_tensor_tensor(out=rcp, in0=small[s][0:n, 0:1].broadcast_to((n, H)), scalar=1e-10,
                                         in1=banks[s][0:n, D:D + H], op0=ALU.mult, op1=ALU.add).then_inc(p1_chain, 1)
                dve.wait_ge(p1_chain, k + 2)
                dve.reciprocal(rcp, rcp).then_inc(p1_chain, 1)
                dve.wait_ge(p1_chain, k + 3)
                dve.tensor_tensor(att[s][0:n, :].rearrange("p (h o) -> p h o", h=H), banks[s][0:n, 0:D].rearrange("p (h o) -> p h o", h=H),
                                  rcp.unsqueeze(2).broadcast_to((n, H, HD)), ALU.mult).then_inc(p1_att, 1)
                dve.wait_ge(p1_x[s], 16 * (tile.turn + 1))
                dve.wait_ge(p1_att, tile.t + 1)
                dve.scalar_tensor_tensor(out=row1[s][0:n, :], in0=x_res[s][0:n, :], scalar=2.0, in1=att[s][0:n, :],
                                         op0=ALU.mult, op1=ALU.add).then_inc(p1_chain, 1)
                moments(tile, row1[s][0:n, :], p1_chain, k + 4, p1_var)
            over_tile_pairs(dve, finish1, normalize(row1, norm1, p1_dev, p1_chain, PER1, p1_out, p1_row))

            dve.wait_ge(p1_turned, TILES)
            dve.memset(sums3[:, 0, :], 0.0).then_inc(zero2, 1)
            dve.wait_ge(root_x, 16)
            dve.scalar_tensor_tensor(out=root_cols[:, KB:2 * KB], in0=root_cols[:, 0:KB], scalar=0.01, in1=root_cols[:, 0:KB],
                                     op0=ALU.mult, op1=ALU.max).then_inc(root_step, 1)
            dve.wait_ge(root_step, 1)
            dve.tensor_copy(root_wide[:, :, :], root_cols[:, KB:2 * KB].unsqueeze(2).broadcast_to((P, KB, P))).then_inc(root_step, 1)
            dve.wait_ge(root_mm, 1)
            dve.tensor_copy(root1_row, banks[4][:, 0:D]).then_inc(root_ok, 1)
            dve.wait_ge(zero2, 2)
            dve.wait_ge(weights_in, 16 * 9)

            def aggregate(r):
                def step(blk):
                    n, rows, s = sum(blk.sizes), blk.rows, blk.slot
                    one_hot(r, blk, hot_step)
                    dve.wait_ge(hot_step, (r - 1) * NBLOCKS + blk.b + 1)
                    h3 = hot[s][0:rows, 0:n * WINDOW].rearrange("p (c j) -> p c j", j=WINDOW)
                    dve.tensor_tensor(h3, h3, w_now[0:rows, bass.ds(blk.chunk, n)].unsqueeze(2).broadcast_to((rows, n, WINDOW)),
                                      ALU.mult).then_inc(R[r]["hot_ready"], 1)
                    for q, size in enumerate(blk.sizes):
                        half = (s + q) % 2
                        base = window_start(blk, q)
                        dve.wait_ge(R[r]["group_done"], blk.group + q + 1)
                        at_least(dve, R[r]["added"], blk.group + q)
                        win = sums3[:, :, bass.ds(base, WINDOW)]
                        new = banks[2 + half][:, 0:KB * WINDOW].rearrange("p (k j) -> p k j", k=KB)
                        dve.tensor_tensor(win, win, new, ALU.add).then_inc(R[r]["added"], 1)
                over_blocks(dve, step)
            aggregate(1)

            dve.wait_ge(root2_mm, 1)
            dve.tensor_tensor(root_cols[:, 2 * KB:3 * KB], banks[4][:, 0:KB], bias_cols[:, 0:KB], ALU.add).then_inc(root2_step, 1)
            dve.wait_ge(root2_step, 1)
            dve.tensor_copy(root_wide[:, :, :], root_cols[:, 2 * KB:3 * KB].unsqueeze(2).broadcast_to((P, KB, P))).then_inc(root2_step, 1)
            dve.wait_ge(root2_mm, 2)
            dve.tensor_copy(root2_row, banks[5][:, 0:D]).then_inc(root2_ok, 1)

            dve.wait_ge(root_ok, 1)

            def leaky_h(ready, free, done):
                def step(tile):
                    n, s = tile.rows, tile.slot
                    dve.wait_ge(ready, 2 * tile.t + 2)
                    at_least(dve, free, tile.t - 1)
                    dve.scalar_tensor_tensor(out=h_t[s][:, :, 0:n], in0=h_pre[s][:, :, 0:n], scalar=0.01, in1=h_pre[s][:, :, 0:n],
                                             op0=ALU.mult, op1=ALU.max).then_inc(done, 1)
                return step

            def finish2(tile):
                n, s = tile.rows, tile.slot
                dve.wait_ge(p2_z, tile.t + 1)
                at_least(dve, p2_out[s], 16 * tile.turn)
                dve.tensor_tensor(row2[s][0:n, :], banks[2 + s][0:n, 0:D], root1_row[0:n, :], ALU.add).then_inc(p2_row, 1)
            over_tile_pairs(dve, leaky_h(p2_act, p2_z, p2_leaky), finish2)
            dve.wait_ge(p2_h, TILES)
            dve.memset(sums3[:, 0, :], 0.0).then_inc(zero3, 1)
            dve.wait_ge(zero3, 2)
            aggregate(2)

            PER3 = 3
            dve.wait_ge(root2_ok, 1)

            def add_root(tile):
                n, s = tile.rows, tile.slot
                dve.wait_ge(p3_mm, tile.t + 1)
                dve.tensor_tensor(pre[s][0:n, :], banks[s][0:n, 0:D], root2_row[0:n, :], ALU.add).then_inc(p3_pre, 1)

            def finish3(tile):
                n, s = tile.rows, tile.slot
                dve.wait_ge(p3_pre, tile.t + 1)
                dve.scalar_tensor_tensor(out=act3[s][0:n, :], in0=pre[s][0:n, :], scalar=0.01, in1=pre[s][0:n, :],
                                         op0=ALU.mult, op1=ALU.max).then_inc(p3_leaky, 1)
                dve.wait_ge(p3_leaky, tile.t + 1)
                dve.wait_ge(p3_x[s], 16 * (tile.turn + 1))
                dve.tensor_tensor(res3[s][0:n, :], act3[s][0:n, :], x1_in[s][0:n, :], ALU.add).then_inc(p3_chain, 1)
                moments(tile, res3[s][0:n, :], p3_chain, tile.turn * 2 * PER3 + s * (PER3 - 1) + 1, p3_var)
            over_tile_pairs(dve, leaky_h(p3_act, p3_mm, p3_in), add_root, finish3, normalize(res3, out3, p3_dev, p3_chain, PER3, p3_out, p3_row))


_INS = ["x", "src", "dst", "edge_weight", "L0_gnn_W", "L0_gnn_a_src", "L0_gnn_a_dst", "L1_gnn_W1", "L1_gnn_b1",
        "L1_gnn_W2", "L1_gnn_b2", "L1_gnn_Wl", "L1_gnn_bl", "L1_gnn_root_idx"]


def kernel(**inputs):
    import concourse.bacc as bacc
    from concourse.bass_utils import run_bass_kernel_spmd

    nc = bacc.Bacc("TRN2", target_bir_lowering=False, num_devices=1)
    arrays, args = {}, {}
    for name in _INS:
        v = np.ascontiguousarray(inputs[name])
        arrays[f"in_{name}"] = v
        args[name] = nc.dram_tensor(f"in_{name}", v.shape, mybir.dt.from_np(v.dtype), kind="ExternalInput").ap()
    out = nc.dram_tensor("out_0", arrays["in_x"].shape, F32, kind="ExternalOutput").ap()
    build(nc, args, out)
    result = run_bass_kernel_spmd(nc, [arrays], core_ids=[0])
    return result.results[0]["out_0"]
```

```python
from collections import namedtuple
from contextlib import ExitStack

import numpy as np
import concourse.bass as bass
from concourse import mybir

F32, I32, BF16 = mybir.dt.float32, mybir.dt.int32, mybir.dt.bfloat16
ALU = mybir.AluOpType
ACT = mybir.ActivationFunctionType
AX_X = mybir.AxisListType.X

P = 128
GROUP = 4
WINDOW = 64
BLOCK_GROUPS = 3
BLOCK = GROUP * BLOCK_GROUPS
EPS = 1e-5
LOWEST = -3.0e38

Block = namedtuple("Block", "b slot turn group chunk sizes rows")


def at_least(eng, sem, value):
    if isinstance(value, int) and value <= 0:
        return
    eng.wait_ge(sem, value)


def build(nc, a, out):
    x, src, dst, edge_weight = a["x"], a["src"], a["dst"], a["edge_weight"]
    N, D = x.shape
    E = src.shape[0]
    H, _, HD = a["L0_gnn_W"].shape
    KB = D // P
    TW = D + H
    XW = D + 2 * H
    PARTS = 3
    AW = PARTS * H
    CHUNKS = -(-E // P)
    LAST_EDGES = E - (CHUNKS - 1) * P
    GROUPS = -(-CHUNKS // GROUP)
    ROWT = -(-CHUNKS // P)
    CPAD = ROWT * P
    FULL_TILES, LAST_NODES = N // P, N % P
    assert D == 2 * P and CHUNKS % GROUP == 1 and LAST_EDGES < P and FULL_TILES % 2 == 1 and LAST_NODES

    TURNS = (CHUNKS - 1) // BLOCK // 2
    TAIL = []
    c, b = TURNS * 2 * BLOCK, TURNS * 2
    while c < CHUNKS:
        full = min(BLOCK, (CHUNKS - 1 - c) // GROUP * GROUP)
        sizes = (GROUP,) * (full // GROUP) if full else (1,)
        TAIL.append(Block(b, b % 2, b // 2, c // GROUP, c, sizes, P if full else LAST_EDGES))
        assert b % 2 == 0 or TAIL[0].sizes == (GROUP,) * len(TAIL[0].sizes)
        c, b = c + sum(sizes), b + 1
    NBLOCKS = b
    assert all(t.group % 2 == t.slot for t in TAIL) and len(TAIL) <= 2

    def full_block(turn, slot):
        b = turn * 2 + slot
        return Block(b, slot, turn, b * BLOCK_GROUPS, b * BLOCK, (GROUP,) * BLOCK_GROUPS, P)

    def over_blocks(eng, step):
        for slot in (0, 1):
            step(full_block(0, slot))
        with eng.Fori(1, TURNS) as turn:
            for slot in (0, 1):
                step(full_block(turn, slot))
        for blk in TAIL:
            step(blk)

    def over_blocks_ahead(eng, step):
        for slot in (0, 1):
            step(full_block(0, slot), full_block(slot, 1 - slot))
        with eng.Fori(1, TURNS - 1) as turn:
            for slot in (0, 1):
                step(full_block(turn, slot), full_block(turn + slot, 1 - slot))
        last = [full_block(TURNS - 1, 0), full_block(TURNS - 1, 1)] + TAIL
        for blk, nxt in zip(last, last[1:] + [None]):
            step(blk, nxt)

    Batch = namedtuple("Batch", "b slot turn n0 tiles rows")

    def over_batches(eng, tiles, *steps):
        turns = FULL_TILES // (2 * tiles)
        assert turns * 2 * tiles == FULL_TILES - 1

        def pair(turn, n0, tiles, rows):
            for step in steps:
                for slot in (0, 1):
                    step(Batch(turn * 2 + slot, slot, turn, n0 + slot * tiles * P, tiles, rows[slot]))
        pair(0, 0, tiles, (P, P))
        with eng.Fori(1, turns) as turn:
            pair(turn, turn * (2 * tiles * P), tiles, (P, P))
        pair(turns, (FULL_TILES - 1) * P, 1, (P, LAST_NODES))

    def batches(tiles):
        return (FULL_TILES - 1) // tiles + 2

    T0, T1 = 2, 4

    def nodes(table, bt):
        return table[bass.ds(bt.n0, (bt.tiles - 1) * P + bt.rows), :].rearrange("(t p) f -> p t f", t=bt.tiles)

    with ExitStack() as ctx:
        def sb(name, shape, dt=F32):
            return ctx.enter_context(nc.sbuf_tensor(name, shape, dt))

        def sem(name):
            return ctx.enter_context(nc.semaphore(name))

        def dram(name, shape, dt=F32):
            return nc.dram_tensor(name, shape, dt, kind="Internal").ap()

        table1 = dram("table1", (N, TW))
        table_dst = dram("table_dst", (N, AW), BF16)
        table2 = dram("table2", (N, D))
        table3 = dram("table3", (N, D))
        w_cols = dram("w_cols", (P, CPAD))

        sums = sb("sums", [P, KB * N])
        heads = sb("heads", [P, N])
        work = sb("work", [P, 2 * BLOCK * TW])
        idx_cols = sb("idx_cols", [P, CPAD + BLOCK], I32)
        rel_cols = sb("rel_cols", [P, CPAD])
        hot = [sb(f"hot{s}", [P, BLOCK * WINDOW]) for s in (0, 1)]
        hot16 = sb("hot16", [P, BLOCK * WINDOW], BF16)
        hotT = [sb(f"hotT{s}", [WINDOW, GROUP * P], BF16) for s in (0, 1)]
        group_sums = [sb(f"group_sums{s}", [WINDOW, TW]) for s in (0, 1)]
        base_i = sb("base_i", [1, GROUPS], I32)
        idx = [sb(f"idx{s}", [P, BLOCK], I32) for s in (0, 1)]
        adst = [sb(f"adst{s}", [WINDOW, BLOCK_GROUPS * AW], BF16) for s in (0, 1)]
        score = sb("score", [P, BLOCK * H])
        leaky = sb("leaky", [P, BLOCK * H])
        prob = [sb(f"prob{s}", [P, BLOCK * H]) for s in (0, 1)]
        top = sb("top", [P, 1])
        run_max = [sb(f"run_max{s}", [1, 1]) for s in (0, 1)]
        neg_max = [sb(f"neg_max{s}", [P, 1]) for s in (0, 1)]
        shrink = [sb(f"shrink{s}", [P, 1]) for s in (0, 1)]
        pos_max = sb("pos_max", [P, 1])
        block_max = sb("block_max", [1, 1])
        ident = sb("ident", [P, P])
        ident16 = sb("ident16", [P, P], BF16)
        iota_f = sb("iota_f", [P, WINDOW])
        ones = sb("ones", [1, P])
        zero_win = sb("zero_win", [P, WINDOW])
        eps_col = sb("eps_col", [P, 1])
        bias_cols = sb("bias_cols", [P, 2 * KB])
        root_i = sb("root_i", [1, 1], I32)
        root_cols = sb("root_cols", [P, 3 * KB])
        small = [sb(f"small{s}", [P, 96]) for s in (0, 1)]

        REC = 32
        sums3 = sums[:, :].rearrange("p (k n) -> p k n", k=KB)
        idx_view = idx_cols[:, :]

        wide = [ctx.enter_context(nc.psum_tensor(f"wide{i}", [P, 1024], F32)) for i in range(4)]
        banks = [wide[i // 2][:, i % 2 * 512:(i % 2 + 1) * 512] for i in range(8)]

        def turned16(half):
            return banks[half][0:WINDOW, 0:GROUP * P // 2].bitcast(BF16)

        def gathered(slot, width):
            return work[:, slot * BLOCK * TW:slot * BLOCK * TW + BLOCK * width].rearrange("p (c f) -> p c f", c=BLOCK)

        def carve(region):
            at = [0]

            def take(width):
                at[0] += width
                assert at[0] <= region.shape[1]
                return region[:, at[0] - width:at[0]]
            return take

        take = carve(sums)
        src_rows, dst_rows = take(CPAD).bitcast(I32), take(CPAD).bitcast(I32)
        w_rows = take(CPAD)
        src_f, dst_f, w_stage = take(CPAD), take(CPAD), take(CPAD)
        base_raw = take(GROUPS).bitcast(I32)
        base_f = take(ROWT * P // GROUP)
        base_all = take(ROWT * P // GROUP)
        a_all = take(2 * D)
        a_prod = take(KB * D)
        take = carve(work)
        w0 = take(KB * XW).rearrange("p (k f) -> p k f", k=KB)
        x_in = [take(T0 * D).rearrange("p (t f) -> p t f", t=T0) for s in (0, 1)]
        x_t = [take(T0 * D).rearrange("p (t k n) -> p t k n", t=T0, k=KB) for s in (0, 1)]
        row0 = [take(T0 * XW).rearrange("p (t f) -> p t f", t=T0) for s in (0, 1)]
        dst16 = [take(T0 * AW // 2).bitcast(BF16).rearrange("p (t a) -> p t a", t=T0) for s in (0, 1)]
        rest = [take(T0 * H).rearrange("p (t h) -> p t h", t=T0) for s in (0, 1)]
        take = carve(work)
        sums_tile = [take(T1 * D).rearrange("p (k n) -> p k n", k=KB) for s in (0, 1)]
        x_res = [take(T1 * D).rearrange("p (t f) -> p t f", t=T1) for s in (0, 1)]
        res1 = [take(T1 * D).rearrange("p (t f) -> p t f", t=T1) for s in (0, 1)]
        heads_tile = [hot[s][:, 0:T1 * P] for s in (0, 1)]
        take = carve(heads)
        w_now = take(CPAD)
        W1s, W2a, W2b, Wla, Wlb = (take(KB * D).rearrange("p (k f) -> p k f", k=KB) for _ in range(5))
        root1_row, root2_row = take(D), take(D)
        root_wide = take(KB * P).rearrange("p (k n) -> p k n", k=KB)
        bl_row = take(D)
        h_t = [take(T1 * D).rearrange("p (k n) -> p k n", k=KB) for s in (0, 1)]
        res3 = [take(T1 * D).rearrange("p (t f) -> p t f", t=T1) for s in (0, 1)]
        row2 = res3
        x1_in = [take(T1 * D).rearrange("p (t f) -> p t f", t=T1) for s in (0, 1)]
        guard_c = [small[s][:, 0:T1] for s in (0, 1)]
        rcp_c = [small[s][:, 8:8 + T1 * H] for s in (0, 1)]
        stats_c = [small[s][:, 40:40 + T1 * 6].rearrange("p (t a) -> p t a", t=T1) for s in (0, 1)]
        mv_c = [small[s][:, 64:64 + T1 * 2].rearrange("p (t a) -> p t a", t=T1) for s in (0, 1)]
        dev_c = [small[s][:, 72:72 + T1] for s in (0, 1)]
        rstd_c = [small[s][:, 80:80 + T1] for s in (0, 1)]
        shift_c = [small[s][:, 88:88 + T1] for s in (0, 1)]

        ident_zero, ident_ok = sem("ident_zero"), sem("ident_ok")
        consts_ok = sem("consts_ok")
        rows_in, rows_zero = sem("rows_in"), sem("rows_zero")
        base_ok, base_mm, base_done = sem("base_ok"), sem("base_mm"), sem("base_done")
        rows_f = sem("rows_f")
        cols_turned, cols_done = sem("cols_turned"), sem("cols_done")
        w_saved = sem("w_saved")
        w0_in, a_in, w0_step, w0_ok = sem("w0_in"), sem("a_in"), sem("w0_step"), sem("w0_ok")
        heads_zero, sums_zero = sem("heads_zero"), sem("sums_zero")

        block = ctx.enter_context(nc.Block())

        waited = sem("waited")

        p0_in = [sem(f"p0_in{s}") for s in (0, 1)]
        p0_turned, p0_copied, p0_mm, p0_row = sem("p0_turned"), sem("p0_copied"), sem("p0_mm"), sem("p0_row")
        p0_split = sem("p0_split")
        p0_out = [sem(f"p0_out{s}") for s in (0, 1)]
        R = []
        for r in range(3):
            R.append({n: sem(f"r{r}_{n}") for n in ("idx_ready", "hot_ready", "added", "group_done", "group_copied", "group_turned")})
            R[r]["rows"] = [sem(f"r{r}_rows{s}") for s in (0, 1)]
        adst_in = [sem(f"adst_in{s}") for s in (0, 1)]
        hot16_ready, hotT_turned, hotT_copied, adst_done = sem("hot16_ready"), sem("hotT_turned"), sem("hotT_copied"), sem("adst_done")
        adst_group = sem("adst_group")
        soft, top_done, top_turned, max_run, max_wide = sem("soft"), sem("top_done"), sem("top_turned"), sem("max_run"), sem("max_wide")
        block_max_done, hot_step = sem("block_max_done"), sem("hot_step")
        neg_ready, prob_ready, scaled = sem("neg_ready"), sem("prob_ready"), sem("scaled")
        p1_x = [sem(f"p1_x{s}") for s in (0, 1)]
        p1_copied, p1_turned, p1_chain, p1_row = sem("p1_copied"), sem("p1_turned"), sem("p1_chain"), sem("p1_row")
        p1_y, p1_rstd, p1_shift, p3_y, p3_rstd, p3_shift = (sem(n) for n in (
            "p1_y", "p1_rstd", "p1_shift", "p3_y", "p3_rstd", "p3_shift"))
        p1_var, p1_dev, p3_var, p3_dev = sem("p1_var"), sem("p1_dev"), sem("p3_var"), sem("p3_dev")
        pos_ready, p1_att = sem("pos_ready"), sem("p1_att")
        p1_out = [sem(f"p1_out{s}") for s in (0, 1)]
        weights_in, root_in, root_x = sem("weights_in"), sem("root_in"), sem("root_x")
        root_step, root_mm, root_ok = sem("root_step"), sem("root_mm"), sem("root_ok")
        zero2, zero3 = sem("zero2"), sem("zero3")
        p2_h, p2_act, p2_z, p2_row = sem("p2_h"), sem("p2_act"), sem("p2_z"), sem("p2_row")
        p2_out = [sem(f"p2_out{s}") for s in (0, 1)]
        p2_leaky, p3_in = sem("p2_leaky"), sem("p3_in")
        root2_mm, root2_step, root2_ok = sem("root2_mm"), sem("root2_step"), sem("root2_ok")
        p3_act, p3_mm, p3_pre, p3_leaky, p3_chain, p3_row = (sem("p3_act"), sem("p3_mm"), sem("p3_pre"), sem("p3_leaky"),
                                                             sem("p3_chain"), sem("p3_row"))
        p3_x = [sem(f"p3_x{s}") for s in (0, 1)]
        p3_out = [sem(f"p3_out{s}") for s in (0, 1)]

        tables = [table1, table2, table3]
        widths = [TW, D, D]
        FT = (CHUNKS - 1) // P
        part = CHUNKS - 1 - FT * P
        N_ROW_DMAS = 3 * 3 + 2

        @block.sync
        def _(sp):
            sp.wait_ge(rows_zero, 3)
            for rows, flat in ((dst_rows, dst), (src_rows, src), (w_rows, edge_weight)):
                r3 = rows.rearrange("p (k e) -> p k e", k=ROWT)
                if FT:
                    sp.dma_start(r3[:, 0:FT, :], flat[0:FT * P * P].rearrange("(k p e) -> p k e", p=P, e=P)).then_inc(rows_in, 16)
                sp.dma_start(r3[0:part, FT, :], flat[FT * P * P:(CHUNKS - 1) * P].rearrange("(p e) -> p e", e=P)).then_inc(rows_in, 16)
                sp.dma_start(r3[part:part + 1, FT, 0:LAST_EDGES],
                             flat[(CHUNKS - 1) * P:E].rearrange("(p e) -> p e", p=1)).then_inc(rows_in, 16)
            span = GROUP * P
            sp.dma_start(base_raw[0:1, 0:GROUPS - 1],
                         dst[0:(GROUPS - 1) * span].rearrange("(o g e) -> o g e", o=1, e=span)[:, :, 0],
                         allow_slow_non_contiguous=True).then_inc(rows_in, 16)
            sp.dma_start(base_raw[0:1, GROUPS - 1:GROUPS],
                         dst[(GROUPS - 1) * span:(GROUPS - 1) * span + 1].rearrange("(o g) -> o g", o=1)).then_inc(rows_in, 16)

            def load_x(bt):
                at_least(sp, p0_turned, bt.b - 1)
                sp.dma_start(x_in[bt.slot][0:bt.rows, 0:bt.tiles, :], nodes(x, bt)).then_inc(p0_in[bt.slot], 16)
            over_batches(sp, T0, load_x)
            sp.wait_ge(cols_done, 3 * ROWT)
            sp.dma_start(w_cols, w_stage).then_inc(w_saved, 16)

            for s in (0, 1):
                sp.wait_ge(p0_out[s], 32 * (batches(T0) // 2))

            def load_adst(blk):
                at_least(sp, adst_done, blk.b - 1)
                for q in range(len(blk.sizes)):
                    base = sp.value_load(base_i[0:1, bass.ds(blk.group + q, 1)], min_val=0, max_val=N - WINDOW)
                    sp.dma_start(adst[blk.slot][:, q * AW:(q + 1) * AW],
                                 table_dst[bass.ds(base, WINDOW), :]).then_inc(adst_in[blk.slot], 16)
            over_blocks(sp, load_adst)

            sp.wait_ge(R[0]["added"], GROUPS)

            def load_res(bt):
                at_least(sp, p1_y, bt.b - 1)
                sp.dma_start(x_res[bt.slot][0:bt.rows, 0:bt.tiles, :], nodes(x, bt)).then_inc(p1_x[bt.slot], 16)
            over_batches(sp, T1, load_res)
            sp.wait_ge(p1_copied, 2 * batches(T1))
            sp.dma_start(w_now, w_cols).then_inc(weights_in, 16)
            for tile, w in ((W1s, a["L1_gnn_W1"]), (W2a, a["L1_gnn_W2"][0:D, :]), (W2b, a["L1_gnn_W2"][D:2 * D, :]),
                            (Wla, a["L1_gnn_Wl"][0:D, :]), (Wlb, a["L1_gnn_Wl"][D:2 * D, :])):
                sp.dma_start(tile, w.rearrange("(k p) f -> p k f", p=P)).then_inc(weights_in, 16)
            sp.dma_start(bl_row[0:1, :], a["L1_gnn_bl"].rearrange("(o f) -> o f", o=1)).then_inc(weights_in, 16)
            sp.dma_start(bias_cols[:, 0:KB], a["L1_gnn_b1"].rearrange("(k p) -> p k", p=P),
                         allow_slow_non_contiguous=True).then_inc(weights_in, 16)
            sp.dma_start(bias_cols[:, KB:2 * KB], a["L1_gnn_b2"].rearrange("(k p) -> p k", p=P),
                         allow_slow_non_contiguous=True).then_inc(weights_in, 16)
            sp.dma_start(root_i[:, :], a["L1_gnn_root_idx"][0:1].rearrange("(o f) -> o f", o=1)).then_inc(root_in, 16)
            sp.wait_ge(root_in, 16)
            for s in (0, 1):
                sp.wait_ge(p1_out[s], 16 * (batches(T1) // 2))
            root = sp.value_load(root_i[0:1, 0:1], min_val=0, max_val=N - 1)
            sp.dma_start(root_cols[:, 0:KB], table2[bass.ds(root, 1), :].rearrange("o (k p) -> p (o k)", p=P),
                         allow_slow_non_contiguous=True).then_inc(root_x, 16)

            sp.wait_ge(R[2]["added"], GROUPS)

            def load_x1(bt):
                at_least(sp, p3_y, bt.b - 1)
                sp.dma_start(x1_in[bt.slot][0:bt.rows, 0:bt.tiles, :], nodes(table2, bt)).then_inc(p3_x[bt.slot], 16)
            over_batches(sp, T1, load_x1)
            for s in (0, 1):
                sp.wait_ge(p3_out[s], 16 * (batches(T1) // 2))

        @block.gpsimd
        def _(pool):
            pool.memset(ident[:, :], 0.0).then_inc(ident_zero, 1)
            pool.wait_ge(ident_zero, 1)
            pool.affine_select(out=ident[:, :], in_=ident[:, :], compare_op=ALU.not_equal, fill=1.0, base=0,
                               pattern=[[-1, P]], channel_multiplier=1).then_inc(ident_ok, 1)
            pool.wait_ge(ident_ok, 1)
            pool.tensor_copy(ident16[:, :], ident[:, :]).then_inc(consts_ok, 1)
            pool.iota(iota_f[:, :], pattern=[[1, WINDOW]], base=0, channel_multiplier=0,
                      allow_small_or_imprecise_dtypes=True).then_inc(consts_ok, 1)
            pool.memset(ones[:, :], 1.0).then_inc(consts_ok, 1)
            pool.memset(zero_win[:, :], 0.0).then_inc(consts_ok, 1)
            pool.memset(eps_col[:, :], EPS).then_inc(consts_ok, 1)
            pool.memset(neg_max[1][:, :], -LOWEST).then_inc(consts_ok, 1)
            pool.memset(run_max[1][:, :], LOWEST).then_inc(consts_ok, 1)
            pool.memset(idx_cols[:, CPAD:CPAD + BLOCK], 0).then_inc(consts_ok, 1)
            pool.memset(heads[:, :], 0.0).then_inc(heads_zero, 1)
            pool.wait_ge(cols_done, 3 * ROWT)
            pool.wait_ge(w_saved, 16)
            pool.wait_ge(w0_ok, 1)
            pool.memset(sums[:, :], 0.0).then_inc(sums_zero, 1)

            def gather(r):
                def step(blk):
                    pool.wait_ge(R[r]["idx_ready"], blk.b + 1)
                    for q, size in enumerate(blk.sizes):
                        at_least(pool, R[r]["added"], (blk.b - 2) * BLOCK_GROUPS + q + 1)
                        pool.sem_inc(waited, 1)
                        for c in range(q * GROUP, q * GROUP + size):
                            pool.indirect_dma_start(
                                gathered(blk.slot, widths[r])[0:blk.rows, c, :], None, tables[r],
                                bass.IndirectOffsetOnAxis(ap=idx[blk.slot][0:blk.rows, c:c + 1], axis=0),
                            ).then_inc(R[r]["rows"][blk.slot], 16)
                over_blocks(pool, step)

            for s in (0, 1):
                pool.wait_ge(p0_out[s], 32 * (batches(T0) // 2))
            gather(0)
            for s in (0, 1):
                pool.wait_ge(p1_out[s], 16 * (batches(T1) // 2))
            pool.memset(sums3[:, 1, :], 0.0).then_inc(zero2, 1)
            gather(1)
            for s in (0, 1):
                pool.wait_ge(p2_out[s], 16 * (batches(T1) // 2))
            pool.wait_ge(root2_ok, 1)
            pool.memset(sums3[:, 1, :], 0.0).then_inc(zero3, 1)
            gather(2)

        @block.scalar
        def _(act):
            for k in range(KB):
                act.dma_start(w0[:, k, 0:D].rearrange("p (h o) -> p h o", h=H),
                              a["L0_gnn_W"][:, k * P:(k + 1) * P, :].rearrange("h p o -> p h o")).then_inc(w0_in, 16)
            for j, name in enumerate(("L0_gnn_a_src", "L0_gnn_a_dst")):
                act.dma_start(a_all[:, j * D:(j + 1) * D],
                              a[name].rearrange("h o u -> (u h o)").partition_broadcast(P)).then_inc(a_in, 16)

            def copy_xt(bt):
                act.wait_ge(p0_turned, bt.b + 1)
                at_least(act, p0_mm, bt.b - 1)
                act.activation(x_t[bt.slot][:, 0:bt.tiles, :, 0:bt.rows],
                               banks[bt.slot].rearrange("p (t k n) -> p t k n", t=T0, k=KB)[:, 0:bt.tiles, :, 0:bt.rows],
                               ACT.Copy).then_inc(p0_copied, 1)

            def store_row0(bt):
                act.wait_ge(p0_split, 4 * bt.b + 4)
                act.dma_start(nodes(table1, bt), row0[bt.slot][0:bt.rows, 0:bt.tiles, 0:TW]).then_inc(p0_out[bt.slot], 16)
                act.dma_start(nodes(table_dst, bt), dst16[bt.slot][0:bt.rows, 0:bt.tiles, :]).then_inc(p0_out[bt.slot], 16)
            over_batches(act, T0, copy_xt, store_row0)

            def copy_idx(r, slot, chunk):
                act.activation(idx[slot][:, :], idx_cols[:, bass.ds(chunk, BLOCK)], ACT.Copy).then_inc(R[r]["idx_ready"], 1)

            def next_idx(r, blk):
                if blk is TAIL[-1]:
                    return
                at_least(act, R[r]["rows"][1 - blk.slot], 16 * BLOCK * (blk.turn + blk.slot))
                act.sem_inc(waited, 1)
                copy_idx(r, 1 - blk.slot, blk.chunk + sum(blk.sizes))

            act.wait_ge(cols_done, 3 * ROWT)
            act.wait_ge(consts_ok, 8)
            copy_idx(0, 0, 0)

            def copy_group(r, blk, q):
                half = (blk.slot + q) % 2
                act.wait_ge(R[r]["group_done"], blk.group + q + 1)
                at_least(act, R[r]["group_turned"], blk.group + q - 1)
                act.sem_inc(waited, 1)
                act.activation(group_sums[half][:, 0:widths[r]], banks[2 + half][0:WINDOW, 0:widths[r]],
                               ACT.Copy).then_inc(R[r]["group_copied"], 1)

            def prepare_act(blk):
                n, rows, s = sum(blk.sizes), blk.rows, blk.slot
                act.wait_ge(R[0]["hot_ready"], blk.b + 1)
                act.sem_inc(waited, 1)
                act.activation(hot16[0:rows, 0:n * WINDOW], hot[s][0:rows, 0:n * WINDOW], ACT.Copy).then_inc(hot16_ready, 1)
                for q, size in enumerate(blk.sizes):
                    half = (s + q) % 2
                    act.wait_ge(hotT_turned, blk.group + q + 1)
                    at_least(act, adst_group, blk.group + q - 1)
                    act.sem_inc(waited, 1)
                    act.activation(hotT[half][:, 0:size * P].rearrange("p (c e) -> p c e", e=P)[:, :, 0:rows],
                                   turned16(half)[:, 0:size * P].rearrange("p (c e) -> p c e", e=P)[:, :, 0:rows],
                                   ACT.Copy).then_inc(hotT_copied, 1)

            def softmax(blk, nxt):
                n, rows, s = sum(blk.sizes), blk.rows, blk.slot
                next_idx(0, blk)
                if nxt:
                    prepare_act(nxt)
                act.wait_ge(max_wide, blk.b + 1)
                act.activation(neg_max[s][:, :], banks[5][:, 448:449], ACT.Copy, scale=-1.0).then_inc(neg_ready, 1)
                act.wait_ge(neg_ready, blk.b + 1)
                act.activation(shrink[s][:, :], neg_max[1 - s][:, :], ACT.Exp, bias=neg_max[s][:, 0:1], scale=-1.0).then_inc(prob_ready, 1)
                act.activation(prob[s][0:rows, 0:n * H], leaky[0:rows, 0:n * H], ACT.Exp,
                               bias=neg_max[s][0:rows, 0:1]).then_inc(prob_ready, 1)
                for q in range(len(blk.sizes)):
                    copy_group(0, blk, q)
            prepare_act(full_block(0, 0))
            over_blocks_ahead(act, softmax)

            act.wait_ge(R[0]["added"], GROUPS)
            last = TAIL[-1].slot
            act.activation(pos_max[:, :], neg_max[last][:, :], ACT.Copy, scale=-1.0).then_inc(pos_ready, 1)
            act.wait_ge(pos_ready, 1)
            act.activation(heads[REC:REC + 1, :], heads[REC:REC + 1, :], ACT.Exp, bias=pos_max[REC:REC + 1, 0:1]).then_inc(pos_ready, 1)
            act.wait_ge(pos_ready, 2)

            def copy_tile(bt):
                at_least(act, p1_turned, bt.b - 1)
                act.sem_inc(waited, 1)
                n = (bt.tiles - 1) * P + bt.rows
                act.activation(sums_tile[bt.slot][:, :, 0:n], sums3[:, :, bass.ds(bt.n0, n)], ACT.Copy).then_inc(p1_copied, 1)
                act.activation(heads_tile[bt.slot][0:REC + 1, 0:n], heads[0:REC + 1, bass.ds(bt.n0, n)], ACT.Copy).then_inc(p1_copied, 1)

            def root_var(var_ready, done):
                def step(bt):
                    s, n, t = bt.slot, bt.rows, bt.tiles
                    act.wait_ge(var_ready, bt.b + 1)
                    act.activation(dev_c[s][0:n, 0:t], mv_c[s][0:n, 0:t, 1], ACT.Sqrt, bias=eps_col[0:n, 0:1]).then_inc(done, 1)
                return step

            def scale_rows(res, shift_ready, done):
                def step(bt):
                    s, n = bt.slot, bt.rows
                    act.wait_ge(shift_ready, bt.b + 1)
                    for t in range(bt.tiles):
                        last = act.activation(res[s][0:n, t, :], res[s][0:n, t, :], ACT.Identity, bias=shift_c[s][0:n, t:t + 1],
                                              scale=rstd_c[s][0:n, t:t + 1])
                    last.then_inc(done, 1)
                return step

            def store(row_ready, table, res, out_sem):
                def step(bt):
                    act.wait_ge(row_ready, bt.b + 1)
                    act.dma_start(nodes(table, bt), res[bt.slot][0:bt.rows, 0:bt.tiles, :]).then_inc(out_sem[bt.slot], 16)
                return step
            over_batches(act, T1, copy_tile, root_var(p1_var, p1_dev), scale_rows(res1, p1_shift, p1_row),
                         store(p1_row, table2, res1, p1_out))
            copy_idx(1, 0, 0)

            act.wait_ge(weights_in, 16 * 9)

            def idx_only(r):
                def step(blk):
                    next_idx(r, blk)
                    for q in range(len(blk.sizes)):
                        copy_group(r, blk, q)
                return step
            over_blocks(act, idx_only(1))

            def act_h(bt):
                act.wait_ge(p2_h, bt.b + 1)
                at_least(act, p2_z, bt.b - 1)
                n = (bt.tiles - 1) * P + bt.rows
                for k in range(KB):
                    act.activation(h_t[bt.slot][:, k, 0:n], wide[bt.slot][:, k * 512:k * 512 + n], ACT.Identity,
                                   bias=bias_cols[:, k:k + 1]).then_inc(p2_act, 1)
            over_batches(act, T1, act_h, store(p2_row, table3, row2, p2_out))
            copy_idx(2, 0, 0)
            over_blocks(act, idx_only(2))

            act.wait_ge(R[2]["added"], GROUPS)

            def act_sums(bt):
                at_least(act, p3_mm, bt.b - 1)
                act.sem_inc(waited, 1)
                n = (bt.tiles - 1) * P + bt.rows
                for k in range(KB):
                    act.activation(h_t[bt.slot][:, k, 0:n], sums3[:, k, bass.ds(bt.n0, n)], ACT.Identity,
                                   bias=bias_cols[:, KB + k:KB + k + 1]).then_inc(p3_act, 1)
            over_batches(act, T1, act_sums, root_var(p3_var, p3_dev), scale_rows(res3, p3_shift, p3_row),
                         store(p3_row, out, res3, p3_out))

        @block.tensor
        def _(pe):
            pe.wait_ge(ident_ok, 1)
            pe.wait_ge(consts_ok, 8)
            pe.wait_ge(base_ok, 1)
            pe.matmul(banks[2][:, 0:ROWT * P // GROUP], ones[0:1, :], base_f[0:1, :], start=True, stop=True).then_inc(base_mm, 1)
            pe.wait_ge(rows_f, 2)
            for k in range(ROWT):
                at_least(pe, cols_done, 3 * (k - 1))
                for j, rows in enumerate((dst_f, src_f, w_rows)):
                    pe.transpose(banks[k % 2][:, j * P:(j + 1) * P], rows[:, k * P:(k + 1) * P], ident[:, :]).then_inc(cols_turned, 1)
            pe.wait_ge(cols_done, 3 * ROWT)

            pe.wait_ge(w0_ok, 1)

            def turn_x(bt):
                pe.wait_ge(p0_in[bt.slot], 16 * (bt.turn + 1))
                at_least(pe, p0_copied, bt.b - 1)
                for t in range(bt.tiles):
                    for k in range(KB):
                        at = (t * KB + k) * P
                        mm = pe.transpose(banks[bt.slot][:, at:at + bt.rows], x_in[bt.slot][0:bt.rows, t, k * P:(k + 1) * P],
                                          ident[0:bt.rows, 0:bt.rows])
                mm.then_inc(p0_turned, 1)

            def mm_x(bt):
                pe.wait_ge(p0_copied, bt.b + 1)
                at_least(pe, p0_row, bt.b - 1)
                for t in range(bt.tiles):
                    for k in range(KB):
                        mm = pe.matmul(wide[1 + bt.slot][0:bt.rows, t * 512:t * 512 + XW], x_t[bt.slot][:, t, k, 0:bt.rows],
                                       w0[:, k, :], start=(k == 0), stop=(k == KB - 1))
                mm.then_inc(p0_mm, 1)
            over_batches(pe, T0, turn_x, mm_x)

            def windows(blk):
                n, rows, s = sum(blk.sizes), blk.rows, blk.slot
                pe.wait_ge(hot16_ready, blk.b + 1)

                def turn(q):
                    half = (s + q) % 2
                    at_least(pe, hotT_copied, blk.group + q - 1)
                    pe.sem_inc(waited, 1)
                    for c in range(blk.sizes[q]):
                        cc = q * GROUP + c
                        mm = pe.transpose(turned16(half)[:, c * P:c * P + rows], hot16[0:rows, cc * WINDOW:(cc + 1) * WINDOW],
                                          ident16[0:rows, 0:rows])
                    mm.then_inc(hotT_turned, 1)

                def pick(q):
                    half = (s + q) % 2
                    pe.wait_ge(hotT_copied, blk.group + q + 1)
                    for c in range(blk.sizes[q]):
                        cc = q * GROUP + c
                        mm = pe.matmul(banks[4 + s][0:rows, cc * AW:(cc + 1) * AW], hotT[half][:, c * P:c * P + rows],
                                       adst[s][:, q * AW:(q + 1) * AW], start=True, stop=True)
                    mm.then_inc(adst_group, 1)
                    return mm
                parts = len(blk.sizes)
                turn(0)
                groups_in_slot = blk.turn * BLOCK_GROUPS + parts
                for q in range(parts):
                    if q + 1 < parts:
                        turn(q + 1)
                    if q == 0:
                        pe.wait_ge(adst_in[s], 16 * groups_in_slot)
                    pick(q)
                pe.wait_ge(adst_group, blk.group + parts)
                pe.sem_inc(adst_done, 1)

            def sum_group(r, blk, q):
                half, rows = (blk.slot + q) % 2, blk.rows
                at_least(pe, R[r]["group_copied"], blk.group + q - 1)
                for c in range(q * GROUP, q * GROUP + blk.sizes[q]):
                    mm = pe.matmul(banks[2 + half][0:WINDOW, 0:widths[r]], hot[blk.slot][0:rows, c * WINDOW:(c + 1) * WINDOW],
                                   gathered(blk.slot, widths[r])[0:rows, c, :], start=(c == q * GROUP),
                                   stop=(c == q * GROUP + blk.sizes[q] - 1))
                mm.then_inc(R[r]["group_done"], 1)

            def turn_group(r, blk, q):
                half = (blk.slot + q) % 2
                pe.wait_ge(R[r]["group_copied"], blk.group + q + 1)
                at_least(pe, R[r]["added"], blk.group + q - 1)
                pe.sem_inc(waited, 1)
                for k in range(KB):
                    mm = pe.transpose(banks[6 + half][:, k * WINDOW:(k + 1) * WINDOW], group_sums[half][:, k * P:(k + 1) * P],
                                      ident[0:WINDOW, 0:WINDOW])
                if widths[r] > D:
                    mm = pe.transpose(banks[6 + half][0:H, KB * WINDOW:(KB + 1) * WINDOW], group_sums[half][:, D:D + H],
                                      ident[0:WINDOW, 0:WINDOW])
                mm.then_inc(R[r]["group_turned"], 1)

            def sum_groups(r, blk, ready):
                parts = len(blk.sizes)
                for q in range(parts):
                    ready(q)
                    sum_group(r, blk, q)
                    if q:
                        turn_group(r, blk, q - 1)
                turn_group(r, blk, parts - 1)

            def attend(blk, nxt):
                n, rows, s = sum(blk.sizes), blk.rows, blk.slot
                if nxt:
                    windows(nxt)
                pe.wait_ge(top_done, blk.b + 1)
                pe.transpose(banks[5][0:1, 320:320 + rows], top[0:rows, 0:1], ident[0:rows, 0:rows]).then_inc(top_turned, 1)
                pe.wait_ge(max_run, blk.b + 1)
                pe.matmul(banks[5][:, 448:449], ones[0:1, :], run_max[s][0:1, 0:1], start=True, stop=True).then_inc(max_wide, 1)
                sum_groups(0, blk, lambda q: pe.wait_ge(scaled, blk.group + q + 1))
            windows(full_block(0, 0))
            over_blocks_ahead(pe, attend)

            def turn_sums(bt):
                pe.wait_ge(p1_copied, 2 * bt.b + 2)
                at_least(pe, p1_att, bt.b - 1)
                n, s = bt.rows, bt.slot
                for t in range(bt.tiles):
                    for k in range(KB):
                        pe.transpose(wide[s][0:n, t * D + k * P:t * D + (k + 1) * P], sums_tile[s][:, k, t * P:t * P + n], ident[:, :])
                    mm = pe.transpose(banks[4 + s][0:n, t * (REC + 1):(t + 1) * (REC + 1)], heads_tile[s][0:REC + 1, t * P:t * P + n],
                                      ident[0:REC + 1, 0:REC + 1])
                mm.then_inc(p1_turned, 1)
            over_batches(pe, T1, turn_sums)

            pe.wait_ge(weights_in, 16 * 9)
            pe.wait_ge(root_step, 2)
            for k in range(KB):
                mm = pe.matmul(banks[4][:, 0:D], root_wide[:, k, :], W2b[:, k, :], start=(k == 0), stop=(k == KB - 1))
            mm.then_inc(root_mm, 1)

            def aggregate(r):
                def step(blk):
                    pe.wait_ge(R[r]["hot_ready"], blk.b + 1)
                    pe.wait_ge(R[r]["rows"][blk.slot], 16 * (blk.turn * BLOCK + sum(blk.sizes)))
                    sum_groups(r, blk, lambda q: None)
                over_blocks(pe, step)
            aggregate(1)

            pe.wait_ge(R[1]["added"], GROUPS)
            pe.wait_ge(root_in, 16)
            root = pe.value_load(root_i[0:1, 0:1], min_val=0, max_val=N - 1)
            for f in range(KB):
                for k in range(KB):
                    mm = pe.matmul(banks[7][:, f:f + 1], W1s[:, k, f * P:(f + 1) * P], sums3[:, k, bass.ds(root, 1)],
                                   start=(k == 0), stop=(k == KB - 1))
            mm.then_inc(root2_mm, 1)
            pe.wait_ge(root2_step, 2)
            for k in range(KB):
                pe.matmul(banks[6][:, 0:D], root_wide[:, k, :], Wlb[:, k, :], start=(k == 0), stop=False)
            pe.matmul(banks[6][:, 0:D], ones[0:1, :], bl_row[0:1, :], start=False, stop=True).then_inc(root2_mm, 1)

            def mm_h(bt):
                at_least(pe, p2_act, 2 * (bt.b - 1))
                n = (bt.tiles - 1) * P + bt.rows
                for f in range(KB):
                    for k in range(KB):
                        mm = pe.matmul(wide[bt.slot][:, f * 512:f * 512 + n], W1s[:, k, f * P:(f + 1) * P],
                                       sums3[:, k, bass.ds(bt.n0, n)], start=(k == 0), stop=(k == KB - 1))
                mm.then_inc(p2_h, 1)

            def mm_nodes(h_ready, out_free, w, half, done):
                def step(bt):
                    s, n = bt.slot, bt.rows
                    pe.wait_ge(h_ready, bt.b + 1)
                    at_least(pe, out_free, bt.b - 1)
                    for t in range(bt.tiles):
                        for k in range(KB):
                            mm = pe.matmul(wide[half + s][0:n, t * D:(t + 1) * D], h_t[s][:, k, t * P:t * P + n], w[:, k, :],
                                           start=(k == 0), stop=(k == KB - 1))
                    mm.then_inc(done, 1)
                return step
            pe.wait_ge(root2_ok, 1)
            over_batches(pe, T1, mm_h, mm_nodes(p2_leaky, p2_row, W2a, 2, p2_z))

            aggregate(2)

            over_batches(pe, T1, mm_nodes(p3_in, p3_pre, Wla, 0, p3_mm))

        @block.vector
        def _(dve):
            for rows in (dst_rows, src_rows, w_rows):
                dve.memset(rows[:, FT * P:CPAD], 0).then_inc(rows_zero, 1)
            dve.memset(base_f[0:1, :], 0.0).then_inc(base_done, 1)
            dve.wait_ge(w0_in, 16 * KB)
            dve.wait_ge(a_in, 32)
            for j in (0, 1):
                for k in range(KB):
                    dve.tensor_tensor(a_prod[:, k * D:(k + 1) * D], w0[:, k, 0:D], a_all[:, j * D:(j + 1) * D], ALU.mult).then_inc(w0_step, 1)
                dve.wait_ge(w0_step, (j + 1) * KB + j)
                red = dve.tensor_reduce(w0[:, :, D + j * H:D + (j + 1) * H],
                                        a_prod.rearrange("p (k h o) -> p k h o", k=KB, h=H), AX_X, ALU.add)
                if j == 0:
                    red.then_inc(w0_step, 1)
                    dve.wait_ge(w0_step, KB + 1)
                else:
                    red.then_inc(w0_ok, 1)
            dve.wait_ge(rows_in, 16 * N_ROW_DMAS)
            dve.wait_ge(base_done, 1)
            dve.tensor_scalar(base_f[0:1, 0:GROUPS], base_raw[0:1, :], float(N - WINDOW), None, ALU.min).then_inc(base_ok, 1)
            dve.tensor_copy(src_f, src_rows).then_inc(rows_f, 1)
            dve.tensor_copy(dst_f, dst_rows).then_inc(rows_f, 1)
            dve.wait_ge(base_ok, 1)
            dve.tensor_copy(base_i[0:1, :], base_f[0:1, 0:GROUPS]).then_inc(base_done, 1)
            dve.wait_ge(base_mm, 1)
            dve.tensor_copy(base_all, banks[2][:, 0:ROWT * P // GROUP]).then_inc(base_done, 1)
            dve.wait_ge(base_done, 3)
            for k in range(ROWT):
                dve.wait_ge(cols_turned, 3 * k + 3)
                bank = banks[k % 2]
                g = P // GROUP
                dve.tensor_tensor(rel_cols[:, k * P:(k + 1) * P].rearrange("p (g c) -> p g c", c=GROUP),
                                  bank[:, 0:P].rearrange("p (g c) -> p g c", c=GROUP),
                                  base_all[:, k * g:(k + 1) * g].unsqueeze(2).broadcast_to((P, g, GROUP)), ALU.subtract).then_inc(cols_done, 1)
                dve.tensor_copy(idx_cols[:, k * P:(k + 1) * P], bank[:, P:2 * P]).then_inc(cols_done, 1)
                dve.tensor_copy(w_stage[:, k * P:(k + 1) * P], bank[:, 2 * P:3 * P]).then_inc(cols_done, 1)

            def copy_row0(bt):
                s, n, t = bt.slot, bt.rows, bt.tiles
                dve.wait_ge(p0_mm, bt.b + 1)
                at_least(dve, p0_out[s], 32 * bt.turn)
                dve.tensor_copy(row0[s][0:n, 0:t, :], wide[1 + s][0:n, :].rearrange("p (t f) -> p t f", t=2)[:, 0:t, 0:XW]).then_inc(p0_row, 1)

            def split_dst(bt):
                s, n, t = bt.slot, bt.rows, bt.tiles
                full = row0[s][0:n, 0:t, D + H:XW]
                part = [dst16[s][0:n, 0:t, j * H:(j + 1) * H] for j in range(PARTS)]
                left = rest[s][0:n, 0:t, :]
                at = 4 * bt.b
                dve.wait_ge(p0_row, bt.b + 1)
                dve.tensor_copy(part[0], full).then_inc(p0_split, 1)
                dve.wait_ge(p0_split, at + 1)
                dve.tensor_tensor(left, full, part[0], ALU.subtract).then_inc(p0_split, 1)
                dve.wait_ge(p0_split, at + 2)
                dve.tensor_copy(part[1], left).then_inc(p0_split, 1)
                dve.wait_ge(p0_split, at + 3)
                dve.tensor_tensor(part[2], left, part[1], ALU.subtract).then_inc(p0_split, 1)
            over_batches(dve, T0, copy_row0, split_dst)

            def one_hot(r, blk, done):
                n, s, rows = sum(blk.sizes), blk.slot, blk.rows
                ins = dve.tensor_tensor(
                    hot[s][0:rows, 0:n * WINDOW].rearrange("p (c j) -> p c j", j=WINDOW),
                    rel_cols[0:rows, bass.ds(blk.chunk, n)].unsqueeze(2).broadcast_to((rows, n, WINDOW)),
                    iota_f[0:rows, :].unsqueeze(1).broadcast_to((rows, n, WINDOW)), ALU.is_equal)
                ins.then_inc(done, 1)

            def window_start(blk, q):
                return dve.value_load(base_i[0:1, bass.ds(blk.group + q, 1)], min_val=0, max_val=N - WINDOW)

            dve.wait_ge(consts_ok, 8)
            dve.wait_ge(sums_zero, 1)
            dve.wait_ge(heads_zero, 1)

            def attend(blk, nxt):
                n, rows, s = sum(blk.sizes), blk.rows, blk.slot
                step = blk.b * 3
                rowsv = gathered(s, TW)[0:rows, 0:n, :]
                if nxt:
                    one_hot(0, nxt, R[0]["hot_ready"])
                sc = score[0:rows, 0:n * H].rearrange("p (c h) -> p c h", h=H)
                dve.wait_ge(adst_group, blk.group + len(blk.sizes))
                dve.tensor_reduce(leaky[0:rows, 0:n * H].rearrange("p (c h) -> p c h", h=H),
                                  banks[4 + s][0:rows, 0:n * AW].rearrange("p (c a h) -> p c h a", a=PARTS, h=H), AX_X, ALU.add).then_inc(soft, 1)
                dve.wait_ge(R[0]["rows"][s], 16 * (blk.turn * BLOCK + n))
                dve.wait_ge(soft, step + 1)
                dve.tensor_tensor(sc, rowsv[:, :, D:D + H], leaky[0:rows, 0:n * H].rearrange("p (c h) -> p c h", h=H),
                                  ALU.add).then_inc(soft, 1)
                dve.wait_ge(soft, step + 2)
                dve.scalar_tensor_tensor(out=leaky[0:rows, 0:n * H], in0=score[0:rows, 0:n * H], scalar=0.2,
                                         in1=score[0:rows, 0:n * H], op0=ALU.mult, op1=ALU.max).then_inc(soft, 1)
                dve.wait_ge(soft, step + 3)
                dve.tensor_reduce(top[0:rows, :], leaky[0:rows, 0:n * H], AX_X, ALU.max).then_inc(top_done, 1)
                dve.wait_ge(top_turned, blk.b + 1)
                dve.tensor_reduce(block_max[0:1, :], banks[5][0:1, 320:320 + rows], AX_X, ALU.max).then_inc(block_max_done, 1)
                dve.wait_ge(block_max_done, blk.b + 1)
                dve.tensor_tensor(run_max[s][:, :], block_max[:, :], run_max[1 - s][:, :], ALU.max).then_inc(max_run, 1)
                dve.wait_ge(prob_ready, blk.b * 2 + 2)
                dve.sem_inc(waited, 1)
                dve.tensor_copy(rowsv[:, :, D:D + H], prob[s][0:rows, 0:n * H].rearrange("p (c h) -> p c h", h=H))
                for q, size in enumerate(blk.sizes):
                    c0 = q * GROUP
                    v = gathered(s, TW)[0:rows, c0:c0 + size, 0:D].rearrange("p c (h o) -> p c h o", h=H)
                    pr = prob[s][0:rows, c0 * H:(c0 + size) * H].rearrange("p (c h) -> p c h", h=H)
                    dve.tensor_tensor(v, v, pr.unsqueeze(3).broadcast_to((rows, size, H, HD)), ALU.mult).then_inc(scaled, 1)
                for q, size in enumerate(blk.sizes):
                    half = (s + q) % 2
                    base = window_start(blk, q)
                    dve.wait_ge(R[0]["group_turned"], blk.group + q + 1)
                    at_least(dve, R[0]["added"], blk.group + q)
                    win = sums3[:, :, bass.ds(base, WINDOW)]
                    new = banks[6 + half][:, 0:KB * WINDOW].rearrange("p (k j) -> p k j", k=KB)
                    hwin, hnew = heads[0:H, bass.ds(base, WINDOW)], banks[6 + half][0:H, KB * WINDOW:(KB + 1) * WINDOW]
                    if q == 0:
                        dve.scalar_tensor_tensor(out=win, in0=win, scalar=shrink[s][:, 0:1], in1=new, op0=ALU.mult, op1=ALU.add)
                        dve.scalar_tensor_tensor(out=hwin, in0=hwin, scalar=shrink[s][0:H, 0:1], in1=hnew, op0=ALU.mult, op1=ALU.add)
                    else:
                        dve.tensor_tensor(win, win, new, ALU.add)
                        dve.tensor_tensor(hwin, hwin, hnew, ALU.add)
                    dve.tensor_scalar(heads[REC:REC + 1, bass.ds(base, WINDOW)], zero_win[REC:REC + 1, :], neg_max[s][REC:REC + 1, 0:1],
                                      None, ALU.add).then_inc(R[0]["added"], 1)
            one_hot(0, full_block(0, 0), R[0]["hot_ready"])
            over_blocks_ahead(dve, attend)

            def moments(bt, y, chain, count, done):
                n, s = bt.rows, bt.slot
                at_least(dve, chain, count)
                for t in range(bt.tiles):
                    last = dve.bn_stats(stats_c[s][0:n, t, :], y[s][0:n, t, :])
                last.then_inc(chain, 1)
                dve.wait_ge(chain, count + 1)
                dve.sem_inc(waited, 1)
                for t in range(bt.tiles):
                    last = dve.bn_aggr(mv_c[s][0:n, t, :], stats_c[s][0:n, t, :])
                last.then_inc(done, 1)

            def shift(dev, rstd_sem, done):
                def step(bt):
                    n, s, t = bt.rows, bt.slot, bt.tiles
                    dve.wait_ge(dev, bt.b + 1)
                    dve.reciprocal(rstd_c[s][0:n, 0:t], dev_c[s][0:n, 0:t]).then_inc(rstd_sem, 1)
                    dve.wait_ge(rstd_sem, bt.b + 1)
                    dve.scalar_tensor_tensor(out=shift_c[s][0:n, 0:t], in0=mv_c[s][0:n, 0:t, 0], scalar=-1.0, in1=rstd_c[s][0:n, 0:t],
                                             op0=ALU.mult, op1=ALU.mult).then_inc(done, 1)
                return step

            def finish1(bt):
                n, s, t = bt.rows, bt.slot, bt.tiles
                k = bt.b * 4
                hv = banks[4 + s][0:n, 0:t * (REC + 1)].rearrange("p (t r) -> p t r", t=t)
                rcp = rcp_c[s][0:n, 0:t * H].rearrange("p (t h) -> p t h", t=t)
                dve.wait_ge(p1_turned, bt.b + 1)
                dve.tensor_copy(guard_c[s][0:n, 0:t], hv[:, :, REC]).then_inc(p1_chain, 1)
                dve.wait_ge(p1_chain, k + 1)
                dve.scalar_tensor_tensor(out=rcp, in0=guard_c[s][0:n, 0:t].unsqueeze(2).broadcast_to((n, t, H)), scalar=1e-10,
                                         in1=hv[:, :, 0:H], op0=ALU.mult, op1=ALU.add).then_inc(p1_chain, 1)
                dve.wait_ge(p1_chain, k + 2)
                dve.reciprocal(rcp, rcp).then_inc(p1_chain, 1)
                dve.wait_ge(p1_chain, k + 3)
                at_least(dve, p1_out[s], 16 * bt.turn)
                dve.tensor_tensor(res1[s][0:n, 0:t, :].rearrange("p t (h o) -> p (t h) o", h=H),
                                  wide[s][0:n, 0:t * D].rearrange("p (a o) -> p a o", o=HD),
                                  rcp_c[s][0:n, 0:t * H].unsqueeze(2).broadcast_to((n, t * H, HD)), ALU.mult).then_inc(p1_att, 1)
                dve.wait_ge(p1_x[s], 16 * (bt.turn + 1))
                dve.wait_ge(p1_att, bt.b + 1)
                dve.scalar_tensor_tensor(out=res1[s][0:n, 0:t, :], in0=x_res[s][0:n, 0:t, :], scalar=2.0, in1=res1[s][0:n, 0:t, :],
                                         op0=ALU.mult, op1=ALU.add).then_inc(p1_y, 1)
                dve.wait_ge(p1_y, bt.b + 1)
                moments(bt, res1, p1_chain, k + 3, p1_var)
            over_batches(dve, T1, finish1, shift(p1_dev, p1_rstd, p1_shift))

            dve.wait_ge(p1_turned, batches(T1))
            dve.memset(sums3[:, 0, :], 0.0).then_inc(zero2, 1)
            dve.wait_ge(root_x, 16)
            dve.scalar_tensor_tensor(out=root_cols[:, KB:2 * KB], in0=root_cols[:, 0:KB], scalar=0.01, in1=root_cols[:, 0:KB],
                                     op0=ALU.mult, op1=ALU.max).then_inc(root_step, 1)
            dve.wait_ge(root_step, 1)
            dve.tensor_copy(root_wide[:, :, :], root_cols[:, KB:2 * KB].unsqueeze(2).broadcast_to((P, KB, P))).then_inc(root_step, 1)
            dve.wait_ge(root_mm, 1)
            dve.tensor_copy(root1_row, banks[4][:, 0:D]).then_inc(root_ok, 1)
            dve.wait_ge(zero2, 2)
            dve.wait_ge(weights_in, 16 * 9)

            def aggregate(r):
                def step(blk):
                    n, rows, s = sum(blk.sizes), blk.rows, blk.slot
                    one_hot(r, blk, hot_step)
                    dve.wait_ge(hot_step, (r - 1) * NBLOCKS + blk.b + 1)
                    h3 = hot[s][0:rows, 0:n * WINDOW].rearrange("p (c j) -> p c j", j=WINDOW)
                    dve.tensor_tensor(h3, h3, w_now[0:rows, bass.ds(blk.chunk, n)].unsqueeze(2).broadcast_to((rows, n, WINDOW)),
                                      ALU.mult).then_inc(R[r]["hot_ready"], 1)
                    for q, size in enumerate(blk.sizes):
                        half = (s + q) % 2
                        base = window_start(blk, q)
                        dve.wait_ge(R[r]["group_turned"], blk.group + q + 1)
                        at_least(dve, R[r]["added"], blk.group + q)
                        win = sums3[:, :, bass.ds(base, WINDOW)]
                        new = banks[6 + half][:, 0:KB * WINDOW].rearrange("p (k j) -> p k j", k=KB)
                        dve.tensor_tensor(win, win, new, ALU.add).then_inc(R[r]["added"], 1)
                over_blocks(dve, step)
            aggregate(1)

            dve.wait_ge(root2_mm, 1)
            dve.tensor_tensor(root_cols[:, 2 * KB:3 * KB], banks[7][:, 0:KB], bias_cols[:, 0:KB], ALU.add).then_inc(root2_step, 1)
            dve.wait_ge(root2_step, 1)
            dve.tensor_copy(root_wide[:, :, :], root_cols[:, 2 * KB:3 * KB].unsqueeze(2).broadcast_to((P, KB, P))).then_inc(root2_step, 1)
            dve.wait_ge(root2_mm, 2)
            dve.tensor_copy(root2_row, banks[6][:, 0:D]).then_inc(root2_ok, 1)

            dve.wait_ge(root_ok, 1)

            def leaky_h(ready, done):
                def step(bt):
                    s, n = bt.slot, (bt.tiles - 1) * P + bt.rows
                    dve.wait_ge(ready, 2 * bt.b + 2)
                    dve.scalar_tensor_tensor(out=h_t[s][:, :, 0:n], in0=h_t[s][:, :, 0:n], scalar=0.01, in1=h_t[s][:, :, 0:n],
                                             op0=ALU.mult, op1=ALU.max).then_inc(done, 1)
                return step

            def add_row(mm, out_sem, half, row, res, done):
                def step(bt):
                    n, s, t = bt.rows, bt.slot, bt.tiles
                    dve.wait_ge(mm, bt.b + 1)
                    at_least(dve, out_sem[s], 16 * bt.turn)
                    dve.tensor_tensor(res[s][0:n, 0:t, :], wide[half + s][0:n, 0:t * D].rearrange("p (t f) -> p t f", t=t),
                                      row[0:n, :].unsqueeze(1).broadcast_to((n, t, D)), ALU.add).then_inc(done, 1)
                return step
            over_batches(dve, T1, leaky_h(p2_act, p2_leaky), add_row(p2_z, p2_out, 2, root1_row, row2, p2_row))
            dve.wait_ge(p2_h, batches(T1))
            dve.memset(sums3[:, 0, :], 0.0).then_inc(zero3, 1)
            dve.wait_ge(zero3, 2)
            aggregate(2)

            dve.wait_ge(root2_ok, 1)
            for s in (0, 1):
                dve.wait_ge(p2_out[s], 16 * (batches(T1) // 2))

            def finish3(bt):
                n, s, t = bt.rows, bt.slot, bt.tiles
                y = res3[s][0:n, 0:t, :]
                dve.wait_ge(p3_pre, bt.b + 1)
                dve.scalar_tensor_tensor(out=y, in0=y, scalar=0.01, in1=y, op0=ALU.mult, op1=ALU.max).then_inc(p3_leaky, 1)
                dve.wait_ge(p3_leaky, bt.b + 1)
                dve.wait_ge(p3_x[s], 16 * (bt.turn + 1))
                dve.tensor_tensor(y, y, x1_in[s][0:n, 0:t, :], ALU.add).then_inc(p3_y, 1)
                dve.wait_ge(p3_y, bt.b + 1)
                moments(bt, res3, p3_chain, bt.b, p3_var)
            over_batches(dve, T1, leaky_h(p3_act, p3_in), add_row(p3_mm, p3_out, 0, root2_row, res3, p3_pre), finish3,
                         shift(p3_dev, p3_rstd, p3_shift))


_INS = ["x", "src", "dst", "edge_weight", "L0_gnn_W", "L0_gnn_a_src", "L0_gnn_a_dst", "L1_gnn_W1", "L1_gnn_b1",
        "L1_gnn_W2", "L1_gnn_b2", "L1_gnn_Wl", "L1_gnn_bl", "L1_gnn_root_idx"]


def kernel(**inputs):
    import concourse.bacc as bacc
    from concourse.bass_utils import run_bass_kernel_spmd

    nc = bacc.Bacc("TRN2", target_bir_lowering=False, num_devices=1)
    arrays, args = {}, {}
    for name in _INS:
        v = np.ascontiguousarray(inputs[name])
        arrays[f"in_{name}"] = v
        args[name] = nc.dram_tensor(f"in_{name}", v.shape, mybir.dt.from_np(v.dtype), kind="ExternalInput").ap()
    out = nc.dram_tensor("out_0", arrays["in_x"].shape, F32, kind="ExternalOutput").ap()
    build(nc, args, out)
    result = run_bass_kernel_spmd(nc, [arrays], core_ids=[0])
    return result.results[0]["out_0"]
```

```python
from collections import namedtuple
from contextlib import ExitStack

import numpy as np
import concourse.bass as bass
from concourse import mybir

F32, I32, BF16 = mybir.dt.float32, mybir.dt.int32, mybir.dt.bfloat16
ALU = mybir.AluOpType
ACT = mybir.ActivationFunctionType
AX_X = mybir.AxisListType.X

P = 128
GROUP = 4
WINDOW = 64
BLOCK_GROUPS = 3
BLOCK = GROUP * BLOCK_GROUPS
EPS = 1e-5
LOWEST = -3.0e38
LAG = 4

Block = namedtuple("Block", "b slot turn group chunk sizes rows")
Batch = namedtuple("Batch", "b slot turn n0 tiles rows")


def at_least(eng, sem, value):
    if isinstance(value, int) and value <= 0:
        return
    eng.wait_ge(sem, value)


def build(nc, a, out):
    x, src, dst, edge_weight = a["x"], a["src"], a["dst"], a["edge_weight"]
    N, D = x.shape
    E = src.shape[0]
    H, _, HD = a["L0_gnn_W"].shape
    KB = D // P
    TW = D + H
    XW = D + 2 * H
    PARTS = 3
    AW = PARTS * H
    CHUNKS = -(-E // P)
    LAST_EDGES = E - (CHUNKS - 1) * P
    GROUPS = -(-CHUNKS // GROUP)
    ROWT = -(-CHUNKS // P)
    CPAD = ROWT * P
    FULL_TILES, LAST_NODES = N // P, N % P
    assert D == 2 * P and CHUNKS % GROUP == 1 and LAST_EDGES < P and FULL_TILES % 2 == 1 and LAST_NODES

    TURNS = (CHUNKS - 1) // BLOCK // 2
    TAIL = []
    c, b = TURNS * 2 * BLOCK, TURNS * 2
    while c < CHUNKS:
        full = min(BLOCK, (CHUNKS - 1 - c) // GROUP * GROUP)
        sizes = (GROUP,) * (full // GROUP) if full else (1,)
        TAIL.append(Block(b, b % 2, b // 2, c // GROUP, c, sizes, P if full else LAST_EDGES))
        assert b % 2 == 0 or TAIL[0].sizes == (GROUP,) * len(TAIL[0].sizes)
        c, b = c + sum(sizes), b + 1
    NBLOCKS = b
    assert all(t.group % 2 == t.slot for t in TAIL) and len(TAIL) <= 2

    def full_block(turn, slot):
        b = turn * 2 + slot
        return Block(b, slot, turn, b * BLOCK_GROUPS, b * BLOCK, (GROUP,) * BLOCK_GROUPS, P)

    def over_blocks(eng, step):
        for slot in (0, 1):
            step(full_block(0, slot))
        with eng.Fori(1, TURNS) as turn:
            for slot in (0, 1):
                step(full_block(turn, slot))
        for blk in TAIL:
            step(blk)

    def over_blocks_ahead(eng, step):
        def around(turn, slot):
            return full_block(turn + (slot - 1), 1 - slot), full_block(turn, slot), full_block(turn + slot, 1 - slot)
        step(None, *around(0, 0)[1:])
        step(*around(0, 1))
        with eng.Fori(1, TURNS - 1) as turn:
            for slot in (0, 1):
                step(*around(turn, slot))
        end = [full_block(TURNS - 2, 1), full_block(TURNS - 1, 0), full_block(TURNS - 1, 1)] + TAIL
        for i in range(1, len(end)):
            step(end[i - 1], end[i], end[i + 1] if i + 1 < len(end) else None)
        step(end[-1], None, None)

    def over_batches(eng, tiles, *steps):
        turns = FULL_TILES // (2 * tiles)
        assert turns * 2 * tiles == FULL_TILES - 1

        def pair(turn, n0, tiles, rows):
            for step in steps:
                for slot in (0, 1):
                    step(Batch(turn * 2 + slot, slot, turn, n0 + slot * tiles * P, tiles, rows[slot]))
        pair(0, 0, tiles, (P, P))
        with eng.Fori(1, turns) as turn:
            pair(turn, turn * (2 * tiles * P), tiles, (P, P))
        pair(turns, (FULL_TILES - 1) * P, 1, (P, LAST_NODES))

    def over_batches_ahead(eng, tiles, first, *steps):
        turns = FULL_TILES // (2 * tiles)

        def pair(steps, turn):
            whole = not (isinstance(turn, int) and turn == turns)
            for step in steps:
                for slot in (0, 1):
                    step(Batch(turn * 2 + slot, slot, turn, turn * (2 * tiles * P) + slot * tiles * P, tiles, P) if whole else
                         Batch(turn * 2 + slot, slot, turn, (FULL_TILES - 1 + slot) * P, 1, (P, LAST_NODES)[slot]))
        pair([first], 0)
        pair([first], 1)
        pair(steps, 0)
        if turns > 2:
            with eng.Fori(1, turns - 1) as turn:
                pair([first], turn + 1)
                pair(steps, turn)
        pair([first], turns)
        pair(steps, turns - 1)
        pair(steps, turns)

    def batches(tiles):
        return (FULL_TILES - 1) // tiles + 2

    def over_chunks(eng, step):
        with eng.Fori(0, CHUNKS - 1) as c:
            step(c, P)
        step(CHUNKS - 1, LAST_EDGES)

    BATCH = -(-N // (2 * TURNS))
    LAST_BATCH = N - (2 * TURNS - 1) * BATCH
    assert 0 < LAST_BATCH <= BATCH <= P and LAG % 2 == 0

    def node_batch(turn, slot):
        b = turn * 2 + slot
        last = isinstance(b, int) and b == 2 * TURNS - 1
        return Batch(b, slot, turn, b * BATCH, 1, LAST_BATCH if last else BATCH)

    def over_blocks_batches(eng, step, *stages):
        behind = LAG // 2
        for turn in range(behind + 1):
            for slot in (0, 1):
                step(full_block(turn, slot), full_block(turn + slot, 1 - slot), node_batch(0, slot) if turn == behind else None)
        with eng.Fori(behind + 1, TURNS - 1) as turn:
            for slot in (0, 1):
                step(full_block(turn, slot), full_block(turn + slot, 1 - slot), node_batch(turn - behind, slot))
        end = [full_block(TURNS - 1, 0), full_block(TURNS - 1, 1)] + TAIL
        for i, blk in enumerate(end):
            step(blk, end[i + 1] if i + 1 < len(end) else None, node_batch(TURNS - 1 - behind, i) if i < 2 else None)
        for turn in range(TURNS - behind, TURNS):
            pair_of_batches(turn, stages)

    def pair_of_batches(turn, stages):
        for stage in stages:
            for slot in (0, 1):
                stage(None, node_batch(turn, slot))

    def over_node_batches(eng, *stages):
        pair_of_batches(0, stages)
        with eng.Fori(1, TURNS - 1) as turn:
            pair_of_batches(turn, stages)
        pair_of_batches(TURNS - 1, stages)

    T0, T1 = 2, 4

    def nodes(table, bt):
        return table[bass.ds(bt.n0, (bt.tiles - 1) * P + bt.rows), :].rearrange("(t p) f -> p t f", t=bt.tiles)

    with ExitStack() as ctx:
        def sb(name, shape, dt=F32):
            return ctx.enter_context(nc.sbuf_tensor(name, shape, dt))

        def sem(name):
            return ctx.enter_context(nc.semaphore(name))

        def dram(name, shape, dt=F32):
            return nc.dram_tensor(name, shape, dt, kind="Internal").ap()

        table1 = dram("table1", (N, TW))
        table_dst = dram("table_dst", (N, AW), BF16)
        table2 = dram("table2", (N, D))
        table3 = dram("table3", (N, D))
        w_cols = dram("w_cols", (P, CPAD))

        sums = sb("sums", [P, KB * N])
        heads = sb("heads", [P, N])
        work = sb("work", [P, 2 * BLOCK * TW])
        idx_cols = sb("idx_cols", [P, CPAD + BLOCK], I32)
        rel_cols = sb("rel_cols", [P, CPAD])
        hot = [sb(f"hot{s}", [P, BLOCK * WINDOW]) for s in (0, 1)]
        hot16 = sb("hot16", [P, BLOCK * WINDOW], BF16)
        hotT = [sb(f"hotT{s}", [WINDOW, GROUP * P], BF16) for s in (0, 1)]
        group_sums = [sb(f"group_sums{s}", [WINDOW, TW]) for s in (0, 1)]
        base_i = sb("base_i", [1, GROUPS], I32)
        span = sb("span", [P, 5])
        peak = sb("peak", [P, H])
        windowed_f = sb("windowed_f", [1, 3])
        windowed_i = sb("windowed_i", [1, 1], I32)
        idx = [sb(f"idx{s}", [P, BLOCK], I32) for s in (0, 1)]
        adst = [sb(f"adst{s}", [WINDOW, BLOCK_GROUPS * AW], BF16) for s in (0, 1)]
        score = sb("score", [P, BLOCK * H])
        leaky = sb("leaky", [P, BLOCK * H])
        top = sb("top", [P, 1])
        run_max = [sb(f"run_max{s}", [1, 1]) for s in (0, 1)]
        neg_max = [sb(f"neg_max{s}", [P, 1]) for s in (0, 1)]
        shrink = [sb(f"shrink{s}", [P, 1]) for s in (0, 1)]
        pos_max = sb("pos_max", [P, 1])
        turned_top = sb("turned_top", [1, P])
        ident = sb("ident", [P, P])
        ident16 = sb("ident16", [P, P], BF16)
        iota_f = sb("iota_f", [P, WINDOW])
        ones = sb("ones", [1, P])
        minus_ones = sb("minus_ones", [1, P])
        zero_win = sb("zero_win", [P, WINDOW])
        eps_col = sb("eps_col", [P, 1])
        bias_cols = sb("bias_cols", [P, 2 * KB])
        root_i = sb("root_i", [1, 1], I32)
        root_cols = sb("root_cols", [P, 3 * KB])
        small = [sb(f"small{s}", [P, 96]) for s in (0, 1)]

        REC = 32
        sums3 = sums[:, :].rearrange("p (k n) -> p k n", k=KB)

        wide = [ctx.enter_context(nc.psum_tensor(f"wide{i}", [P, 1024], F32)) for i in range(4)]
        banks = [wide[i // 2][:, i % 2 * 512:(i % 2 + 1) * 512] for i in range(8)]

        def turned16(half):
            return banks[half][0:WINDOW, 0:GROUP * P // 2].bitcast(BF16)

        def gathered(slot, width):
            return work[:, slot * BLOCK * TW:slot * BLOCK * TW + BLOCK * width].rearrange("p (c f) -> p c f", c=BLOCK)

        def carve(region):
            at = [0]

            def take(width):
                at[0] += width
                assert at[0] <= region.shape[1]
                return region[:, at[0] - width:at[0]]
            return take

        take = carve(sums)
        src_rows, dst_rows = take(CPAD).bitcast(I32), take(CPAD).bitcast(I32)
        w_rows = take(CPAD)
        src_f, dst_f, w_stage = take(CPAD), take(CPAD), take(CPAD)
        base_raw = take(GROUPS).bitcast(I32)
        base_f = take(ROWT * P // GROUP)
        base_all = take(ROWT * P // GROUP)
        a_all = take(2 * D)
        a_prod = take(KB * D)
        take = carve(work)
        w0 = take(KB * XW).rearrange("p (k f) -> p k f", k=KB)
        x_in = [take(T0 * D).rearrange("p (t f) -> p t f", t=T0) for s in (0, 1)]
        x_t = [take(T0 * D).rearrange("p (t k n) -> p t k n", t=T0, k=KB) for s in (0, 1)]
        row0 = [take(T0 * XW).rearrange("p (t f) -> p t f", t=T0) for s in (0, 1)]
        dst16 = [take(T0 * AW // 2).bitcast(BF16).rearrange("p (t a) -> p t a", t=T0) for s in (0, 1)]
        rest = [take(T0 * H).rearrange("p (t h) -> p t h", t=T0) for s in (0, 1)]
        plain_src, plain_dst = idx[0][:, 0:1], idx[1][:, 0:1]
        plain_row = hot[0][0:1, 0:P].bitcast(I32)
        plain_adst = hot16[:, 0:AW]
        due = hot[1][0:1, 0:2 * TURNS - LAG]
        take = carve(work)
        sums_tile = [take(T1 * D).rearrange("p (k n) -> p k n", k=KB) for s in (0, 1)]
        x_res = [take(T1 * D).rearrange("p (t f) -> p t f", t=T1) for s in (0, 1)]
        res1 = [take(T1 * D).rearrange("p (t f) -> p t f", t=T1) for s in (0, 1)]
        heads_tile = [hot[s][:, 0:T1 * P] for s in (0, 1)]
        take = carve(heads)
        w_now = take(CPAD)
        W1s, W2a, W2b, Wla, Wlb = (take(KB * D).rearrange("p (k f) -> p k f", k=KB) for _ in range(5))
        root1_row, root2_row = take(D), take(D)
        root_wide = take(KB * P).rearrange("p (k n) -> p k n", k=KB)
        bl_row = take(D)
        h_t = [take(KB * P).rearrange("p (k n) -> p k n", k=KB) for s in (0, 1)]
        row2 = [take(D).rearrange("p (t f) -> p t f", t=1) for s in (0, 1)]
        res3 = [take(D).rearrange("p (t f) -> p t f", t=1) for s in (0, 1)]
        x1_in = [take(D).rearrange("p (t f) -> p t f", t=1) for s in (0, 1)]
        guard_c = [small[s][:, 0:T1] for s in (0, 1)]
        rcp_c = [small[s][:, 8:8 + T1 * H] for s in (0, 1)]
        stats_c = [small[s][:, 40:40 + T1 * 6].rearrange("p (t a) -> p t a", t=T1) for s in (0, 1)]
        mv_c = [small[s][:, 64:64 + T1 * 2].rearrange("p (t a) -> p t a", t=T1) for s in (0, 1)]
        dev_c = [small[s][:, 72:72 + T1] for s in (0, 1)]
        rstd_c = [small[s][:, 80:80 + T1] for s in (0, 1)]
        shift_c = [small[s][:, 88:88 + T1] for s in (0, 1)]

        ident_zero, ident_ok = sem("ident_zero"), sem("ident_ok")
        consts_ok = sem("consts_ok")
        rows_in, rows_zero = sem("rows_in"), sem("rows_zero")
        base_ok, base_mm, base_done = sem("base_ok"), sem("base_mm"), sem("base_done")
        rows_f = sem("rows_f")
        cols_turned, cols_done = sem("cols_turned"), sem("cols_done")
        w_saved = sem("w_saved")
        w0_in, a_in, w0_step, w0_ok = sem("w0_in"), sem("a_in"), sem("w0_step"), sem("w0_ok")
        heads_zero, sums_zero = sem("heads_zero"), sem("sums_zero")

        block = ctx.enter_context(nc.Block())

        waited = sem("waited")

        p0_in = [sem(f"p0_in{s}") for s in (0, 1)]
        p0_turned, p0_copied, p0_mm, p0_row = sem("p0_turned"), sem("p0_copied"), sem("p0_mm"), sem("p0_row")
        p0_split = sem("p0_split")
        p0_out = [sem(f"p0_out{s}") for s in (0, 1)]
        R = []
        for r in range(3):
            R.append({n: sem(f"r{r}_{n}") for n in ("idx_ready", "hot_ready", "added", "group_done", "group_copied", "group_turned")})
            R[r]["rows"] = [sem(f"r{r}_rows{s}") for s in (0, 1)]
        adst_in = [sem(f"adst_in{s}") for s in (0, 1)]
        hot16_ready, hotT_turned, hotT_copied, adst_done = sem("hot16_ready"), sem("hotT_turned"), sem("hotT_copied"), sem("adst_done")
        adst_group = sem("adst_group")
        soft, top_done, top_turned, max_run, max_wide = sem("soft"), sem("top_done"), sem("top_turned"), sem("max_run"), sem("max_wide")
        hot_step = sem("hot_step")
        neg_ready, prob_ready, scaled = sem("neg_ready"), sem("prob_ready"), sem("scaled")
        span_step, span_turned, windowed_ok = sem("span_step"), sem("span_turned"), sem("windowed_ok")
        span_chain = sem("span_chain")
        plain_free, plain_ids_in, plain_src_ready, plain_rows, plain_chain, plain_peaked, plain_scored, plain_weighed = (
            sem("plain_" + n) for n in ("free", "ids_in", "src_ready", "rows", "chain", "peaked", "scored", "weighed"))
        plain_scaled, plain_turned, plain_added = sem("plain_scaled"), sem("plain_turned"), sem("plain_added")
        p1_x = [sem(f"p1_x{s}") for s in (0, 1)]
        p1_copied, p1_turned, p1_chain, p1_row = sem("p1_copied"), sem("p1_turned"), sem("p1_chain"), sem("p1_row")
        p1_y, p1_rstd, p1_shift, p3_y, p3_rstd, p3_shift = (sem(n) for n in (
            "p1_y", "p1_rstd", "p1_shift", "p3_y", "p3_rstd", "p3_shift"))
        p1_var, p1_dev, p3_var, p3_dev = sem("p1_var"), sem("p1_dev"), sem("p3_var"), sem("p3_dev")
        pos_ready, p1_att = sem("pos_ready"), sem("p1_att")
        p1_out = [sem(f"p1_out{s}") for s in (0, 1)]
        weights_in, root_in, root_x = sem("weights_in"), sem("root_in"), sem("root_x")
        root_step, root_mm, root_ok = sem("root_step"), sem("root_mm"), sem("root_ok")
        cleared = sem("cleared")
        p2_h, p2_act, p2_z, p2_row = sem("p2_h"), sem("p2_act"), sem("p2_z"), sem("p2_row")
        p2_out = [sem(f"p2_out{s}") for s in (0, 1)]
        p2_leaky, p3_in = sem("p2_leaky"), sem("p3_in")
        root2_mm, root2_step, root2_ok = sem("root2_mm"), sem("root2_step"), sem("root2_ok")
        p3_act, p3_mm, p3_pre, p3_leaky, p3_chain, p3_row = (sem("p3_act"), sem("p3_mm"), sem("p3_pre"), sem("p3_leaky"),
                                                             sem("p3_chain"), sem("p3_row"))
        p3_x = [sem(f"p3_x{s}") for s in (0, 1)]
        p3_out = [sem(f"p3_out{s}") for s in (0, 1)]

        tables = [table1, table2, table3]
        widths = [TW, D, D]
        FT = (CHUNKS - 1) // P
        part = CHUNKS - 1 - FT * P
        N_ROW_DMAS = 3 * 3 + 2

        def by_windows(eng, windows, plain):
            eng.wait_ge(windowed_ok, 1)
            windowed = eng.value_load(windowed_i[0:1, 0:1], min_val=0, max_val=1)
            with eng.If(windowed > 0):
                windows()
            with eng.Else():
                plain()
            eng.end_ifs()

        @block.sync
        def _(sp):
            sp.wait_ge(rows_zero, 3)
            for rows, flat in ((dst_rows, dst), (src_rows, src), (w_rows, edge_weight)):
                r3 = rows.rearrange("p (k e) -> p k e", k=ROWT)
                if FT:
                    sp.dma_start(r3[:, 0:FT, :], flat[0:FT * P * P].rearrange("(k p e) -> p k e", p=P, e=P)).then_inc(rows_in, 16)
                sp.dma_start(r3[0:part, FT, :], flat[FT * P * P:(CHUNKS - 1) * P].rearrange("(p e) -> p e", e=P)).then_inc(rows_in, 16)
                sp.dma_start(r3[part:part + 1, FT, 0:LAST_EDGES],
                             flat[(CHUNKS - 1) * P:E].rearrange("(p e) -> p e", p=1)).then_inc(rows_in, 16)
            span = GROUP * P
            sp.dma_start(base_raw[0:1, 0:GROUPS - 1],
                         dst[0:(GROUPS - 1) * span].rearrange("(o g e) -> o g e", o=1, e=span)[:, :, 0],
                         allow_slow_non_contiguous=True).then_inc(rows_in, 16)
            sp.dma_start(base_raw[0:1, GROUPS - 1:GROUPS],
                         dst[(GROUPS - 1) * span:(GROUPS - 1) * span + 1].rearrange("(o g) -> o g", o=1)).then_inc(rows_in, 16)

            def load_x(bt):
                at_least(sp, p0_turned, bt.b - 1)
                sp.dma_start(x_in[bt.slot][0:bt.rows, 0:bt.tiles, :], nodes(x, bt)).then_inc(p0_in[bt.slot], 16)
            over_batches(sp, T0, load_x)
            sp.wait_ge(cols_done, 3 * ROWT)
            sp.dma_start(w_cols, w_stage).then_inc(w_saved, 16)

            for s in (0, 1):
                sp.wait_ge(p0_out[s], 32 * (batches(T0) // 2))

            def load_adst(blk):
                at_least(sp, adst_done, blk.b - 1)
                for q in range(len(blk.sizes)):
                    base = sp.value_load(base_i[0:1, bass.ds(blk.group + q, 1)], min_val=0, max_val=N - WINDOW)
                    sp.dma_start(adst[blk.slot][:, q * AW:(q + 1) * AW],
                                 table_dst[bass.ds(base, WINDOW), :]).then_inc(adst_in[blk.slot], 16)

            def plain_ids(i):
                def step(c, rows):
                    sp.wait_ge(plain_free, c + (i * (CHUNKS + 1) + 1))
                    edges = dst[bass.ds(c * P, rows)]
                    sp.dma_start(plain_dst[0:rows, :], edges.rearrange("(p o) -> p o", o=1)).then_inc(plain_ids_in, 16)
                    sp.dma_start(plain_row[:, 0:rows], edges.rearrange("(o e) -> o e", o=1)).then_inc(plain_ids_in, 16)
                return lambda: over_chunks(sp, step)

            def plain_ids0():
                plain_ids(0)()
                plain_ids(1)()
            by_windows(sp, lambda: over_blocks(sp, load_adst), plain_ids0)

            sp.wait_ge(R[0]["added"], GROUPS)

            def load_res(bt):
                at_least(sp, p1_y, bt.b - 1)
                sp.dma_start(x_res[bt.slot][0:bt.rows, 0:bt.tiles, :], nodes(x, bt)).then_inc(p1_x[bt.slot], 16)
            over_batches(sp, T1, load_res)
            sp.wait_ge(p1_copied, 2 * batches(T1))
            sp.dma_start(w_now, w_cols).then_inc(weights_in, 16)
            for tile, w in ((W1s, a["L1_gnn_W1"]), (W2a, a["L1_gnn_W2"][0:D, :]), (W2b, a["L1_gnn_W2"][D:2 * D, :]),
                            (Wla, a["L1_gnn_Wl"][0:D, :]), (Wlb, a["L1_gnn_Wl"][D:2 * D, :])):
                sp.dma_start(tile, w.rearrange("(k p) f -> p k f", p=P)).then_inc(weights_in, 16)
            sp.dma_start(bl_row[0:1, :], a["L1_gnn_bl"].rearrange("(o f) -> o f", o=1)).then_inc(weights_in, 16)
            sp.dma_start(bias_cols[:, 0:KB], a["L1_gnn_b1"].rearrange("(k p) -> p k", p=P),
                         allow_slow_non_contiguous=True).then_inc(weights_in, 16)
            sp.dma_start(bias_cols[:, KB:2 * KB], a["L1_gnn_b2"].rearrange("(k p) -> p k", p=P),
                         allow_slow_non_contiguous=True).then_inc(weights_in, 16)
            sp.dma_start(root_i[:, :], a["L1_gnn_root_idx"][0:1].rearrange("(o f) -> o f", o=1)).then_inc(root_in, 16)
            sp.wait_ge(root_in, 16)
            for s in (0, 1):
                sp.wait_ge(p1_out[s], 16 * (batches(T1) // 2))
            root = sp.value_load(root_i[0:1, 0:1], min_val=0, max_val=N - 1)
            sp.dma_start(root_cols[:, 0:KB], table2[bass.ds(root, 1), :].rearrange("o (k p) -> p (o k)", p=P),
                         allow_slow_non_contiguous=True).then_inc(root_x, 16)

            def load_x1(blk, bt):
                at_least(sp, p3_y, bt.b - 1)
                sp.dma_start(x1_in[bt.slot][0:bt.rows, 0:bt.tiles, :], nodes(table2, bt)).then_inc(p3_x[bt.slot], 16)

            def plain_ids3():
                plain_ids(3)()
                over_node_batches(sp, load_x1)
            by_windows(sp, lambda: None, plain_ids(2))
            by_windows(sp, lambda: over_node_batches(sp, load_x1), plain_ids3)
            for s in (0, 1):
                sp.wait_ge(p3_out[s], 16 * TURNS)

        @block.gpsimd
        def _(pool):
            pool.memset(ident[:, :], 0.0).then_inc(ident_zero, 1)
            pool.wait_ge(ident_zero, 1)
            pool.affine_select(out=ident[:, :], in_=ident[:, :], compare_op=ALU.not_equal, fill=1.0, base=0,
                               pattern=[[-1, P]], channel_multiplier=1).then_inc(ident_ok, 1)
            pool.wait_ge(ident_ok, 1)
            pool.tensor_copy(ident16[:, :], ident[:, :]).then_inc(consts_ok, 1)
            pool.iota(iota_f[:, :], pattern=[[1, WINDOW]], base=0, channel_multiplier=0,
                      allow_small_or_imprecise_dtypes=True).then_inc(consts_ok, 1)
            pool.iota(due, pattern=[[BATCH, 2 * TURNS - LAG]], base=BATCH, channel_multiplier=0,
                      allow_small_or_imprecise_dtypes=True).then_inc(consts_ok, 1)
            pool.memset(ones[:, :], 1.0).then_inc(consts_ok, 1)
            pool.memset(minus_ones[:, :], -1.0).then_inc(consts_ok, 1)
            pool.memset(zero_win[:, :], 0.0).then_inc(consts_ok, 1)
            pool.memset(eps_col[:, :], EPS).then_inc(consts_ok, 1)
            pool.memset(neg_max[1][:, :], -LOWEST).then_inc(consts_ok, 1)
            pool.memset(run_max[1][:, :], LOWEST).then_inc(consts_ok, 1)
            pool.memset(idx_cols[:, CPAD:CPAD + BLOCK], 0).then_inc(consts_ok, 1)
            pool.memset(heads[:, :], 0.0).then_inc(heads_zero, 1)
            pool.wait_ge(cols_done, 3 * ROWT)
            pool.wait_ge(w_saved, 16)
            pool.wait_ge(w0_ok, 1)
            pool.memset(sums[:, :], 0.0).then_inc(sums_zero, 1)

            def gather(r):
                def step(blk):
                    pool.wait_ge(R[r]["idx_ready"], blk.b + 1)
                    for q, size in enumerate(blk.sizes):
                        at_least(pool, R[r]["group_done"], (blk.b - 2) * BLOCK_GROUPS + q + 1)
                        pool.sem_inc(waited, 1)
                        for c in range(q * GROUP, q * GROUP + size):
                            pool.indirect_dma_start(
                                gathered(blk.slot, widths[r])[0:blk.rows, c, :], None, tables[r],
                                bass.IndirectOffsetOnAxis(ap=idx[blk.slot][0:blk.rows, c:c + 1], axis=0),
                            ).then_inc(R[r]["rows"][blk.slot], 16)
                return lambda: over_blocks(pool, step)

            def plain_gather(i, r):
                def step(c, rows):
                    pool.wait_ge(plain_src_ready, c + (i * CHUNKS + 1))
                    pool.sem_inc(waited, 1)
                    pool.indirect_dma_start(gathered(0, widths[r])[0:rows, 0, :], None, tables[r],
                                            bass.IndirectOffsetOnAxis(ap=plain_src[0:rows, :], axis=0)).then_inc(plain_rows, 16)
                    if r == 0:
                        pool.wait_ge(plain_ids_in, c * 32 + (i * CHUNKS + 1) * 32)
                        pool.sem_inc(waited, 1)
                        pool.indirect_dma_start(plain_adst[0:rows, :], None, table_dst,
                                                bass.IndirectOffsetOnAxis(ap=plain_dst[0:rows, :], axis=0)).then_inc(plain_rows, 16)
                return lambda: over_chunks(pool, step)

            def plain_gather0():
                plain_gather(0, 0)()
                plain_gather(1, 0)()

            for s in (0, 1):
                pool.wait_ge(p0_out[s], 32 * (batches(T0) // 2))
            by_windows(pool, gather(0), plain_gather0)
            for s in (0, 1):
                pool.wait_ge(p1_out[s], 16 * (batches(T1) // 2))
            by_windows(pool, gather(1), plain_gather(2, 1))
            for s in (0, 1):
                pool.wait_ge(p2_out[s], 16 * TURNS)
            by_windows(pool, gather(2), plain_gather(3, 2))

        @block.scalar
        def _(act):
            for k in range(KB):
                act.dma_start(w0[:, k, 0:D].rearrange("p (h o) -> p h o", h=H),
                              a["L0_gnn_W"][:, k * P:(k + 1) * P, :].rearrange("h p o -> p h o")).then_inc(w0_in, 16)
            for j, name in enumerate(("L0_gnn_a_src", "L0_gnn_a_dst")):
                act.dma_start(a_all[:, j * D:(j + 1) * D],
                              a[name].rearrange("h o u -> (u h o)").partition_broadcast(P)).then_inc(a_in, 16)

            def copy_xt(bt):
                act.wait_ge(p0_turned, bt.b + 1)
                at_least(act, p0_mm, bt.b - 1)
                act.activation(x_t[bt.slot][:, 0:bt.tiles, :, 0:bt.rows],
                               banks[bt.slot].rearrange("p (t k n) -> p t k n", t=T0, k=KB)[:, 0:bt.tiles, :, 0:bt.rows],
                               ACT.Copy).then_inc(p0_copied, 1)

            def store_row0(bt):
                act.wait_ge(p0_split, 4 * bt.b + 4)
                act.dma_start(nodes(table1, bt), row0[bt.slot][0:bt.rows, 0:bt.tiles, 0:TW]).then_inc(p0_out[bt.slot], 16)
                act.dma_start(nodes(table_dst, bt), dst16[bt.slot][0:bt.rows, 0:bt.tiles, :]).then_inc(p0_out[bt.slot], 16)
            over_batches_ahead(act, T0, copy_xt, store_row0)

            def copy_idx(r, slot, chunk):
                act.activation(idx[slot][:, :], idx_cols[:, bass.ds(chunk, BLOCK)], ACT.Copy).then_inc(R[r]["idx_ready"], 1)

            def first_idx(r):
                copy_idx(r, 0, 0)
                copy_idx(r, 1, BLOCK)

            def later_idx(r, blk, nxt):
                if not nxt or nxt is TAIL[-1]:
                    return
                act.wait_ge(R[r]["rows"][blk.slot], 16 * (blk.turn * BLOCK + sum(blk.sizes)))
                act.sem_inc(waited, 1)
                copy_idx(r, blk.slot, nxt.chunk + sum(nxt.sizes))

            act.wait_ge(cols_done, 3 * ROWT)
            act.wait_ge(consts_ok, 10)

            def copy_group(r, blk, q):
                half = (blk.slot + q) % 2
                act.wait_ge(R[r]["group_done"], blk.group + q + 1)
                at_least(act, R[r]["group_turned"], blk.group + q - 1)
                act.sem_inc(waited, 1)
                act.activation(group_sums[half][:, 0:widths[r]], banks[2 + half][0:WINDOW, 0:widths[r]],
                               ACT.Copy).then_inc(R[r]["group_copied"], 1)

            def copy_turned(blk, q):
                half, rows, size = (blk.slot + q) % 2, blk.rows, blk.sizes[q]
                act.wait_ge(hotT_turned, blk.group + q + 1)
                at_least(act, adst_group, blk.group + q - 1)
                act.sem_inc(waited, 1)
                act.activation(hotT[half][:, 0:size * P].rearrange("p (c e) -> p c e", e=P)[:, :, 0:rows],
                               turned16(half)[:, 0:size * P].rearrange("p (c e) -> p c e", e=P)[:, :, 0:rows],
                               ACT.Copy).then_inc(hotT_copied, 1)

            def copy_hot(blk):
                n, rows = sum(blk.sizes), blk.rows
                act.wait_ge(hot16_ready, blk.b + 1)
                act.sem_inc(waited, 1)
                act.activation(hot[blk.slot][0:rows, 0:n * WINDOW], hot16[0:rows, 0:n * WINDOW], ACT.Copy).then_inc(R[0]["hot_ready"], 1)

            def softmax(last, blk, nxt):
                if blk:
                    n, rows, s = sum(blk.sizes), blk.rows, blk.slot
                    act.wait_ge(max_wide, blk.b + 1)
                    act.sem_inc(waited, 1)
                    act.activation(neg_max[s][:, :], banks[5][:, 448:449], ACT.Copy).then_inc(neg_ready, 1)
                    act.wait_ge(neg_ready, blk.b + 1)
                    act.activation(gathered(s, TW)[0:rows, 0:n, D:D + H], leaky[0:rows, 0:n * H].rearrange("p (c h) -> p c h", h=H), ACT.Exp,
                                   bias=neg_max[s][0:rows, 0:1]).then_inc(prob_ready, 1)
                    act.activation(shrink[s][:, :], neg_max[1 - s][:, :], ACT.Exp, bias=neg_max[s][:, 0:1], scale=-1.0).then_inc(prob_ready, 1)
                    later_idx(0, blk, nxt)
                if last:
                    copy_group(0, last, len(last.sizes) - 1)
                for q in range(BLOCK_GROUPS):
                    if nxt and q < len(nxt.sizes):
                        copy_turned(nxt, q)
                    if blk and 0 < q < len(blk.sizes):
                        copy_group(0, blk, q - 1)
                if nxt:
                    copy_hot(nxt)

            def attend_windows():
                first_idx(0)
                for q in range(BLOCK_GROUPS):
                    copy_turned(full_block(0, 0), q)
                copy_hot(full_block(0, 0))
                over_blocks_ahead(act, softmax)

            def plain_copy(i, r):
                def step(c, rows):
                    act.wait_ge(plain_free, c + (i * (CHUNKS + 1) + 1))
                    act.sem_inc(waited, 1)
                    act.activation(plain_src, idx_cols[:, bass.ds(c, 1)], ACT.Copy).then_inc(plain_src_ready, 1)
                    if i == 1:
                        act.wait_ge(plain_scored, c + 1)
                        act.sem_inc(waited, 1)
                        act.activation(gathered(0, TW)[0:rows, 0, D:D + H], leaky[0:rows, 0:H], ACT.Exp,
                                       bias=neg_max[TAIL[-1].slot][0:rows, 0:1]).then_inc(plain_weighed, 1)
                return lambda: over_chunks(act, step)

            def attend_plain():
                plain_copy(0, 0)()
                act.wait_ge(max_wide, 1)
                neg = neg_max[TAIL[-1].slot]
                act.activation(neg[:, :], banks[5][:, 448:449], ACT.Copy).then_inc(neg_ready, 1)
                act.wait_ge(neg_ready, 1)
                act.activation(heads[REC:REC + 1, :], heads[REC:REC + 1, :], ACT.Identity, bias=neg[REC:REC + 1, 0:1]).then_inc(neg_ready, 1)
                act.wait_ge(neg_ready, 2)
                plain_copy(1, 0)()
            by_windows(act, attend_windows, attend_plain)

            act.wait_ge(R[0]["added"], GROUPS)
            last = TAIL[-1].slot
            act.activation(pos_max[:, :], neg_max[last][:, :], ACT.Copy, scale=-1.0).then_inc(pos_ready, 1)
            act.wait_ge(pos_ready, 1)
            EARLY = 4 * T1 * P

            def guard(n0, n1):
                row = heads[REC:REC + 1, n0:n1]
                act.activation(row, row, ACT.Exp, bias=pos_max[REC:REC + 1, 0:1]).then_inc(pos_ready, 1)
            guard(0, EARLY)
            act.wait_ge(pos_ready, 2)

            def copy_tile(bt):
                at_least(act, p1_turned, bt.b - 1)
                act.sem_inc(waited, 1)
                n = (bt.tiles - 1) * P + bt.rows
                act.activation(sums_tile[bt.slot][:, :, 0:n], sums3[:, :, bass.ds(bt.n0, n)], ACT.Copy).then_inc(p1_copied, 1)
                act.activation(heads_tile[bt.slot][0:REC + 1, 0:n], heads[0:REC + 1, bass.ds(bt.n0, n)], ACT.Copy).then_inc(p1_copied, 1)
                if isinstance(bt.b, int) and bt.b == 3:
                    guard(EARLY, N)
                    act.wait_ge(pos_ready, 3)

            def root_var(var_ready, done):
                def step(bt):
                    s, n, t = bt.slot, bt.rows, bt.tiles
                    act.wait_ge(var_ready, bt.b + 1)
                    act.activation(dev_c[s][0:n, 0:t], mv_c[s][0:n, 0:t, 1], ACT.Sqrt, bias=eps_col[0:n, 0:1]).then_inc(done, 1)
                return step

            def scale_rows(res, shift_ready, done):
                def step(bt):
                    s, n = bt.slot, bt.rows
                    act.wait_ge(shift_ready, bt.b + 1)
                    for t in range(bt.tiles):
                        last = act.activation(res[s][0:n, t, :], res[s][0:n, t, :], ACT.Identity, bias=shift_c[s][0:n, t:t + 1],
                                              scale=rstd_c[s][0:n, t:t + 1])
                    last.then_inc(done, 1)
                return step

            def store(row_ready, table, res, out_sem):
                def step(bt):
                    act.wait_ge(row_ready, bt.b + 1)
                    act.dma_start(nodes(table, bt), res[bt.slot][0:bt.rows, 0:bt.tiles, :]).then_inc(out_sem[bt.slot], 16)
                return step
            norm1 = (root_var(p1_var, p1_dev), scale_rows(res1, p1_shift, p1_row), store(p1_row, table2, res1, p1_out))

            def finish_rows(bt):
                for step in norm1:
                    step(bt)
            over_batches_ahead(act, T1, copy_tile, finish_rows)

            act.wait_ge(weights_in, 16 * 9)

            def act_h(blk, bt):
                n = bt.rows
                act.wait_ge(p2_h, bt.b + 1)
                at_least(act, p2_z, bt.b - 1)
                act.sem_inc(waited, 1)
                for k in range(KB):
                    act.activation(h_t[bt.slot][:, k, 0:n], banks[bt.slot][:, k * P:k * P + n], ACT.Identity,
                                   bias=bias_cols[:, k:k + 1]).then_inc(p2_act, 1)

            def act_sums(blk, bt):
                n = bt.rows
                act.wait_ge(R[2]["added"], blk.group - 1 if blk else GROUPS)
                act.sem_inc(waited, 1)
                at_least(act, p3_mm, bt.b - 1)
                act.sem_inc(waited, 1)
                for k in range(KB):
                    act.activation(h_t[bt.slot][:, k, 0:n], sums3[:, k, bass.ds(bt.n0, n)], ACT.Identity,
                                   bias=bias_cols[:, KB + k:KB + k + 1]).then_inc(p3_act, 1)

            def act_round(r, i, features, *finish):
                def step(blk, nxt, bt):
                    later_idx(r, blk, nxt)
                    if bt:
                        features(blk, bt)
                    for q in range(min(2, len(blk.sizes))):
                        copy_group(r, blk, q)
                    if bt:
                        for stage in finish[:-2]:
                            stage(bt)
                    if len(blk.sizes) > 2:
                        copy_group(r, blk, 2)
                    if bt:
                        for stage in finish[-2:]:
                            stage(bt)

                def finish_batch(blk, bt):
                    for stage in finish:
                        stage(bt)

                def windows():
                    first_idx(r)
                    over_blocks_batches(act, step, features, finish_batch)

                def plain():
                    plain_copy(i, r)()
                    over_node_batches(act, features, finish_batch)
                by_windows(act, windows, plain)
            act_round(1, 2, act_h, store(p2_row, table3, row2, p2_out))
            act_round(2, 3, act_sums, root_var(p3_var, p3_dev), scale_rows(res3, p3_shift, p3_row), store(p3_row, out, res3, p3_out))

        @block.tensor
        def _(pe):
            pe.wait_ge(ident_ok, 1)
            pe.wait_ge(consts_ok, 10)
            pe.wait_ge(base_ok, 1)
            pe.matmul(banks[2][:, 0:ROWT * P // GROUP], ones[0:1, :], base_f[0:1, :], start=True, stop=True).then_inc(base_mm, 1)
            pe.wait_ge(rows_f, 2)
            for k in range(ROWT):
                at_least(pe, cols_done, 3 * (k - 1))
                for j, rows in enumerate((dst_f, src_f, w_rows)):
                    pe.transpose(banks[k % 2][:, j * P:(j + 1) * P], rows[:, k * P:(k + 1) * P], ident[:, :]).then_inc(cols_turned, 1)
            pe.wait_ge(cols_done, 3 * ROWT)

            pe.wait_ge(w0_ok, 1)

            def turn_x(bt):
                pe.wait_ge(p0_in[bt.slot], 16 * (bt.turn + 1))
                at_least(pe, p0_copied, bt.b - 1)
                for t in range(bt.tiles):
                    for k in range(KB):
                        at = (t * KB + k) * P
                        mm = pe.transpose(banks[bt.slot][:, at:at + bt.rows], x_in[bt.slot][0:bt.rows, t, k * P:(k + 1) * P],
                                          ident[0:bt.rows, 0:bt.rows])
                mm.then_inc(p0_turned, 1)

            def mm_x(bt):
                pe.wait_ge(p0_copied, bt.b + 1)
                at_least(pe, p0_row, bt.b - 1)
                for t in range(bt.tiles):
                    for k in range(KB):
                        mm = pe.matmul(wide[1 + bt.slot][0:bt.rows, t * 512:t * 512 + XW], x_t[bt.slot][:, t, k, 0:bt.rows],
                                       w0[:, k, :], start=(k == 0), stop=(k == KB - 1))
                mm.then_inc(p0_mm, 1)
            over_batches_ahead(pe, T0, turn_x, mm_x)
            pe.wait_ge(span_step, 3)
            pe.transpose(banks[7][0:1, 0:P], span[:, 4:5], ident[:, :]).then_inc(span_turned, 1)

            def turn_hot(blk, q):
                half, rows = (blk.slot + q) % 2, blk.rows
                if q == 0:
                    pe.wait_ge(hot16_ready, blk.b + 1)
                at_least(pe, hotT_copied, blk.group + q - 1)
                pe.sem_inc(waited, 1)
                for c in range(blk.sizes[q]):
                    cc = q * GROUP + c
                    mm = pe.transpose(turned16(half)[:, c * P:c * P + rows], hot16[0:rows, cc * WINDOW:(cc + 1) * WINDOW],
                                      ident16[0:rows, 0:rows])
                mm.then_inc(hotT_turned, 1)

            def pick(blk, q):
                half, rows, s = (blk.slot + q) % 2, blk.rows, blk.slot
                if q == 0:
                    pe.wait_ge(adst_in[s], 16 * (blk.turn * BLOCK_GROUPS + len(blk.sizes)))
                pe.wait_ge(hotT_copied, blk.group + q + 1)
                for c in range(blk.sizes[q]):
                    cc = q * GROUP + c
                    mm = pe.matmul(banks[4 + s][0:rows, cc * AW:(cc + 1) * AW], hotT[half][:, c * P:c * P + rows],
                                   adst[s][:, q * AW:(q + 1) * AW], start=True, stop=True)
                mm.then_inc(adst_group, 1)
                if q == len(blk.sizes) - 1:
                    pe.wait_ge(adst_group, blk.group + q + 1)
                    pe.sem_inc(adst_done, 1)

            def sum_group(r, blk, q):
                half, rows = (blk.slot + q) % 2, blk.rows
                at_least(pe, R[r]["group_copied"], blk.group + q - 1)
                for c in range(q * GROUP, q * GROUP + blk.sizes[q]):
                    mm = pe.matmul(banks[2 + half][0:WINDOW, 0:widths[r]], hot[blk.slot][0:rows, c * WINDOW:(c + 1) * WINDOW],
                                   gathered(blk.slot, widths[r])[0:rows, c, :], start=(c == q * GROUP),
                                   stop=(c == q * GROUP + blk.sizes[q] - 1))
                mm.then_inc(R[r]["group_done"], 1)

            def turn_group(r, blk, q):
                half = (blk.slot + q) % 2
                pe.wait_ge(R[r]["group_copied"], blk.group + q + 1)
                at_least(pe, R[r]["added"], blk.group + q - 1)
                pe.sem_inc(waited, 1)
                for k in range(KB):
                    mm = pe.transpose(banks[6 + half][:, k * WINDOW:(k + 1) * WINDOW], group_sums[half][:, k * P:(k + 1) * P],
                                      ident[0:WINDOW, 0:WINDOW])
                if widths[r] > D:
                    mm = pe.transpose(banks[6 + half][0:H, KB * WINDOW:(KB + 1) * WINDOW], group_sums[half][:, D:D + H],
                                      ident[0:WINDOW, 0:WINDOW])
                mm.then_inc(R[r]["group_turned"], 1)

            def attend(last, blk, nxt):
                def sum_scaled(q):
                    if blk and q < len(blk.sizes) - 1:
                        pe.wait_ge(scaled, blk.group + q + 1)
                        sum_group(0, blk, q)
                if blk:
                    rows, s = blk.rows, blk.slot
                    pe.wait_ge(top_done, blk.b + 1)
                    pe.transpose(banks[5][0:1, 320:320 + rows], top[0:rows, 0:1], ident[0:rows, 0:rows]).then_inc(top_turned, 1)
                if last and len(last.sizes) > 1:
                    turn_group(0, last, len(last.sizes) - 2)
                if blk:
                    pe.wait_ge(max_run, blk.b + 1)
                    at_least(pe, neg_ready, blk.b)
                    pe.sem_inc(waited, 1)
                    pe.matmul(banks[5][:, 448:449], minus_ones[0:1, :], run_max[s][0:1, 0:1], start=True, stop=True).then_inc(max_wide, 1)
                if last:
                    q = len(last.sizes) - 1
                    pe.wait_ge(scaled, last.group + q + 1)
                    sum_group(0, last, q)
                ahead = len(nxt.sizes) if nxt else 0
                for q in range(min(2, ahead)):
                    turn_hot(nxt, q)
                if blk:
                    pe.wait_ge(R[0]["hot_ready"], blk.b + 1)
                sum_scaled(0)
                if ahead:
                    pick(nxt, 0)
                if ahead > 2:
                    turn_hot(nxt, 2)
                if last:
                    turn_group(0, last, len(last.sizes) - 1)
                for q in range(1, ahead):
                    pick(nxt, q)
                sum_scaled(1)
                for q in range(len(blk.sizes) - 2 if blk else 0):
                    turn_group(0, blk, q)

            def attend_windows():
                first = full_block(0, 0)
                turn_hot(first, 0)
                for q in range(BLOCK_GROUPS):
                    if q + 1 < BLOCK_GROUPS:
                        turn_hot(first, q + 1)
                    pick(first, q)
                over_blocks_ahead(pe, attend)

            def plain_turn(i, r):
                def step(c, rows):
                    pe.wait_ge(plain_scaled, c + ((i - 1) * CHUNKS + 1))
                    pe.sem_inc(waited, 1)
                    v = gathered(0, widths[r])[0:rows, 0, :]
                    for k in range(KB):
                        mm = pe.transpose(banks[6][:, k * P:k * P + rows], v[:, k * P:(k + 1) * P], ident[0:rows, 0:rows])
                    if r == 0:
                        mm = pe.transpose(banks[7][0:H, 0:rows], v[:, D:D + H], ident[0:rows, 0:rows])
                    mm.then_inc(plain_turned, 1)
                return lambda: over_chunks(pe, step)

            def attend_plain():
                pe.wait_ge(top_done, 1)
                pe.transpose(banks[5][0:1, 320:320 + P], top[:, 0:1], ident[:, :]).then_inc(top_turned, 1)
                pe.wait_ge(max_run, 1)
                pe.matmul(banks[5][:, 448:449], minus_ones[0:1, :], run_max[0][0:1, 0:1], start=True, stop=True).then_inc(max_wide, 1)
                plain_turn(1, 0)()
            by_windows(pe, attend_windows, attend_plain)

            def turn_sums(bt):
                pe.wait_ge(p1_copied, 2 * bt.b + 2)
                at_least(pe, p1_y, bt.b - 1)
                n, s = bt.rows, bt.slot
                for t in range(bt.tiles):
                    for k in range(KB):
                        pe.transpose(wide[s][0:n, t * D + k * P:t * D + (k + 1) * P], sums_tile[s][:, k, t * P:t * P + n], ident[:, :])
                    mm = pe.transpose(banks[4 + s][0:n, t * (REC + 1):(t + 1) * (REC + 1)], heads_tile[s][0:REC + 1, t * P:t * P + n],
                                      ident[0:REC + 1, 0:REC + 1])
                mm.then_inc(p1_turned, 1)
            over_batches(pe, T1, turn_sums)

            pe.wait_ge(weights_in, 16 * 9)
            pe.wait_ge(root_step, 2)
            for k in range(KB):
                mm = pe.matmul(banks[4][:, 0:D], root_wide[:, k, :], W2b[:, k, :], start=(k == 0), stop=(k == KB - 1))
            mm.then_inc(root_mm, 1)

            def mm_h(blk, bt):
                n, s = bt.rows, bt.slot
                pe.wait_ge(R[1]["added"], blk.group - 1 if blk else GROUPS)
                pe.sem_inc(waited, 1)
                at_least(pe, p2_act, 2 * (bt.b - 1))
                for f in range(KB):
                    for k in range(KB):
                        mm = pe.matmul(banks[s][:, f * P:f * P + n], W1s[:, k, f * P:(f + 1) * P],
                                       sums3[:, k, bass.ds(bt.n0, n)], start=(k == 0), stop=(k == KB - 1))
                mm.then_inc(p2_h, 1)

            def mm_nodes(h_ready, out_free, w, done):
                def step(bt):
                    s, n = bt.slot, bt.rows
                    pe.wait_ge(h_ready, bt.b + 1)
                    at_least(pe, out_free, bt.b - 1)
                    pe.sem_inc(waited, 1)
                    for k in range(KB):
                        mm = pe.matmul(banks[4 + s][0:n, 0:D], h_t[s][:, k, 0:n], w[:, k, :],
                                       start=(k == 0), stop=(k == KB - 1))
                    mm.then_inc(done, 1)
                return step

            def pe_round(r, i, features, product):
                def step(blk, nxt, bt):
                    n = len(blk.sizes)
                    if bt and features:
                        features(blk, bt)
                    pe.wait_ge(R[r]["hot_ready"], blk.b + 1)
                    pe.wait_ge(R[r]["rows"][blk.slot], 16 * (blk.turn * BLOCK + sum(blk.sizes)))
                    for q in range(min(n, 2)):
                        sum_group(r, blk, q)
                    if n > 1:
                        turn_group(r, blk, 0)
                    if bt:
                        product(bt)
                    if n > 2:
                        sum_group(r, blk, 2)
                        turn_group(r, blk, 1)
                    turn_group(r, blk, n - 1)

                stages = ([features] if features else []) + [lambda blk, bt: product(bt)]

                def plain():
                    plain_turn(i, r)()
                    over_node_batches(pe, *stages)
                by_windows(pe, lambda: over_blocks_batches(pe, step, *stages), plain)
            pe_round(1, 2, mm_h, mm_nodes(p2_leaky, p2_row, W2a, p2_z))

            pe.wait_ge(R[1]["added"], GROUPS)
            pe.wait_ge(root_in, 16)
            root = pe.value_load(root_i[0:1, 0:1], min_val=0, max_val=N - 1)
            for f in range(KB):
                for k in range(KB):
                    mm = pe.matmul(banks[7][:, f:f + 1], W1s[:, k, f * P:(f + 1) * P], sums3[:, k, bass.ds(root, 1)],
                                   start=(k == 0), stop=(k == KB - 1))
            mm.then_inc(root2_mm, 1)
            pe.wait_ge(root2_step, 2)
            for k in range(KB):
                pe.matmul(banks[6][:, 0:D], root_wide[:, k, :], Wlb[:, k, :], start=(k == 0), stop=False)
            pe.matmul(banks[6][:, 0:D], ones[0:1, :], bl_row[0:1, :], start=False, stop=True).then_inc(root2_mm, 1)

            pe_round(2, 3, None, mm_nodes(p3_in, p3_pre, Wla, p3_mm))

        @block.vector
        def _(dve):
            for rows in (dst_rows, src_rows, w_rows):
                dve.memset(rows[:, FT * P:CPAD], 0).then_inc(rows_zero, 1)
            dve.memset(base_f[0:1, :], 0.0).then_inc(base_done, 1)
            dve.wait_ge(w0_in, 16 * KB)
            dve.wait_ge(a_in, 32)
            for j in (0, 1):
                for k in range(KB):
                    dve.tensor_tensor(a_prod[:, k * D:(k + 1) * D], w0[:, k, 0:D], a_all[:, j * D:(j + 1) * D], ALU.mult).then_inc(w0_step, 1)
                dve.wait_ge(w0_step, (j + 1) * KB + j)
                red = dve.tensor_reduce(w0[:, :, D + j * H:D + (j + 1) * H],
                                        a_prod.rearrange("p (k h o) -> p k h o", k=KB, h=H), AX_X, ALU.add)
                if j == 0:
                    red.then_inc(w0_step, 1)
                    dve.wait_ge(w0_step, KB + 1)
                else:
                    red.then_inc(w0_ok, 1)
            dve.wait_ge(rows_in, 16 * N_ROW_DMAS)
            dve.wait_ge(base_done, 1)
            dve.tensor_scalar(base_f[0:1, 0:GROUPS], base_raw[0:1, :], float(N - WINDOW), None, ALU.min).then_inc(base_ok, 1)
            dve.tensor_copy(src_f, src_rows).then_inc(rows_f, 1)
            dve.tensor_copy(dst_f, dst_rows).then_inc(rows_f, 1)
            dve.wait_ge(base_ok, 1)
            dve.tensor_copy(base_i[0:1, :], base_f[0:1, 0:GROUPS]).then_inc(base_done, 1)
            dve.wait_ge(base_mm, 1)
            dve.tensor_copy(base_all, banks[2][:, 0:ROWT * P // GROUP]).then_inc(base_done, 1)
            dve.wait_ge(base_done, 3)
            for k in range(ROWT):
                dve.wait_ge(cols_turned, 3 * k + 3)
                bank = banks[k % 2]
                g = P // GROUP
                dve.tensor_tensor(rel_cols[:, k * P:(k + 1) * P].rearrange("p (g c) -> p g c", c=GROUP),
                                  bank[:, 0:P].rearrange("p (g c) -> p g c", c=GROUP),
                                  base_all[:, k * g:(k + 1) * g].unsqueeze(2).broadcast_to((P, g, GROUP)), ALU.subtract).then_inc(cols_done, 1)
                dve.tensor_copy(idx_cols[:, k * P:(k + 1) * P], bank[:, P:2 * P]).then_inc(cols_done, 1)
                dve.tensor_copy(w_stage[:, k * P:(k + 1) * P], bank[:, 2 * P:3 * P]).then_inc(cols_done, 1)

            def copy_row0(bt):
                s, n, t = bt.slot, bt.rows, bt.tiles
                dve.wait_ge(p0_mm, bt.b + 1)
                at_least(dve, p0_out[s], 32 * bt.turn)
                dve.tensor_copy(row0[s][0:n, 0:t, :], wide[1 + s][0:n, :].rearrange("p (t f) -> p t f", t=2)[:, 0:t, 0:XW]).then_inc(p0_row, 1)

            def split_dst(bt):
                s, n, t = bt.slot, bt.rows, bt.tiles
                full = row0[s][0:n, 0:t, D + H:XW]
                part = [dst16[s][0:n, 0:t, j * H:(j + 1) * H] for j in range(PARTS)]
                left = rest[s][0:n, 0:t, :]
                at = 4 * bt.b
                dve.wait_ge(p0_row, bt.b + 1)
                dve.tensor_copy(part[0], full).then_inc(p0_split, 1)
                dve.wait_ge(p0_split, at + 1)
                dve.tensor_tensor(left, full, part[0], ALU.subtract).then_inc(p0_split, 1)
                dve.wait_ge(p0_split, at + 2)
                dve.tensor_copy(part[1], left).then_inc(p0_split, 1)
                dve.wait_ge(p0_split, at + 3)
                dve.tensor_tensor(part[2], left, part[1], ALU.subtract).then_inc(p0_split, 1)
            over_batches(dve, T0, copy_row0, split_dst)

            dve.wait_ge(consts_ok, 10)
            dve.memset(span[:, :], 0.0).then_inc(span_step, 1)
            dve.wait_ge(span_step, 1)
            first = LAG * BLOCK_GROUPS - 1
            dve.tensor_tensor(due, due, base_i[0:1, first:first + due.shape[1] * BLOCK_GROUPS:BLOCK_GROUPS], ALU.subtract)
            dve.tensor_reduce(span[:, 0:1], rel_cols[:, 0:CHUNKS - 1], AX_X, ALU.max)
            dve.tensor_copy(span[0:LAST_EDGES, 1:2], rel_cols[0:LAST_EDGES, CHUNKS - 1:CHUNKS])
            dve.tensor_reduce(span[:, 2:3], rel_cols[:, 0:CHUNKS - 1], AX_X, ALU.min)
            dve.tensor_copy(span[0:LAST_EDGES, 3:4], rel_cols[0:LAST_EDGES, CHUNKS - 1:CHUNKS])
            dve.tensor_tensor(hot[0][0:1, 0:GROUPS - 1], base_i[0:1, 0:GROUPS - 1], base_i[0:1, 1:GROUPS], ALU.subtract).then_inc(span_step, 1)
            dve.wait_ge(span_step, 2)
            dve.tensor_scalar(span[:, 2:4], span[:, 2:4], -float(WINDOW), None, ALU.mult)
            dve.tensor_reduce(windowed_f[0:1, 2:3], due, AX_X, ALU.max)
            dve.tensor_reduce(windowed_f[0:1, 1:2], hot[0][0:1, 0:GROUPS - 1], AX_X, ALU.max).then_inc(span_chain, 1)
            dve.wait_ge(span_chain, 1)
            dve.tensor_reduce(span[:, 4:5], span[:, 0:4], AX_X, ALU.max).then_inc(span_step, 1)
            dve.tensor_scalar(windowed_f[0:1, 1:3], windowed_f[0:1, 1:3], float(WINDOW), None, ALU.mult)
            dve.wait_ge(span_turned, 1)
            dve.tensor_reduce(windowed_f[0:1, 0:1], banks[7][0:1, 0:P], AX_X, ALU.max).then_inc(span_chain, 1)
            dve.wait_ge(span_chain, 2)
            dve.tensor_reduce(span[0:1, 0:1], windowed_f[0:1, :], AX_X, ALU.max).then_inc(span_chain, 1)
            dve.wait_ge(span_chain, 3)
            dve.tensor_scalar(span[0:1, 1:2], span[0:1, 0:1], WINDOW - 0.5, None, ALU.is_lt).then_inc(span_chain, 1)
            dve.wait_ge(span_chain, 4)
            dve.tensor_copy(windowed_i[:, :], span[0:1, 1:2]).then_inc(windowed_ok, 1)

            def one_hot(r, blk, to, done):
                n, rows = sum(blk.sizes), blk.rows
                ins = dve.tensor_tensor(
                    to[0:rows, 0:n * WINDOW].rearrange("p (c j) -> p c j", j=WINDOW),
                    rel_cols[0:rows, bass.ds(blk.chunk, n)].unsqueeze(2).broadcast_to((rows, n, WINDOW)),
                    iota_f[0:rows, :].unsqueeze(1).broadcast_to((rows, n, WINDOW)), ALU.is_equal)
                ins.then_inc(done, 1)

            def window_start(blk, q):
                return dve.value_load(base_i[0:1, bass.ds(blk.group + q, 1)], min_val=0, max_val=N - WINDOW)

            dve.wait_ge(consts_ok, 10)
            dve.wait_ge(sums_zero, 1)
            dve.wait_ge(heads_zero, 1)

            def hot16_rows(blk):
                n, rows = sum(blk.sizes), blk.rows
                at_least(dve, hotT_turned, blk.group)
                at_least(dve, R[0]["hot_ready"], blk.b)
                dve.sem_inc(waited, 1)
                one_hot(0, blk, hot16, hot16_ready)

            def add_group(blk, q):
                s, half = blk.slot, (blk.slot + q) % 2
                base = window_start(blk, q)
                dve.wait_ge(R[0]["group_turned"], blk.group + q + 1)
                at_least(dve, R[0]["added"], blk.group + q)
                win = sums3[:, :, bass.ds(base, WINDOW)]
                new = banks[6 + half][:, 0:KB * WINDOW].rearrange("p (k j) -> p k j", k=KB)
                hwin, hnew = heads[0:H, bass.ds(base, WINDOW)], banks[6 + half][0:H, KB * WINDOW:(KB + 1) * WINDOW]
                if q == 0:
                    dve.scalar_tensor_tensor(out=win, in0=win, scalar=shrink[s][:, 0:1], in1=new, op0=ALU.mult, op1=ALU.add)
                    dve.scalar_tensor_tensor(out=hwin, in0=hwin, scalar=shrink[s][0:H, 0:1], in1=hnew, op0=ALU.mult, op1=ALU.add)
                else:
                    dve.tensor_tensor(win, win, new, ALU.add)
                    dve.tensor_tensor(hwin, hwin, hnew, ALU.add)
                dve.tensor_scalar(heads[REC:REC + 1, bass.ds(base, WINDOW)], zero_win[REC:REC + 1, :], neg_max[s][REC:REC + 1, 0:1],
                                  None, ALU.add).then_inc(R[0]["added"], 1)

            def attend(last, blk, nxt):
                if blk:
                    n, rows, s = sum(blk.sizes), blk.rows, blk.slot
                    step = blk.b * 3
                    rowsv = gathered(s, TW)[0:rows, 0:n, :]
                    sc = score[0:rows, 0:n * H].rearrange("p (c h) -> p c h", h=H)
                    picked = leaky[0:rows, 0:n * H].rearrange("p (c h) -> p c h", h=H)
                    dve.wait_ge(adst_group, blk.group + len(blk.sizes))
                    dve.tensor_reduce(picked, banks[4 + s][0:rows, 0:n * AW].rearrange("p (c a h) -> p c h a", a=PARTS, h=H),
                                      AX_X, ALU.add).then_inc(soft, 1)
                    dve.wait_ge(R[0]["rows"][s], 16 * (blk.turn * BLOCK + n))
                    dve.wait_ge(soft, step + 1)
                    dve.tensor_tensor(sc, rowsv[:, :, D:D + H], picked, ALU.add).then_inc(soft, 1)
                    dve.wait_ge(soft, step + 2)
                    dve.scalar_tensor_tensor(out=leaky[0:rows, 0:n * H], in0=score[0:rows, 0:n * H], scalar=0.2,
                                             in1=score[0:rows, 0:n * H], op0=ALU.mult, op1=ALU.max).then_inc(soft, 1)
                    dve.wait_ge(soft, step + 3)
                    dve.tensor_reduce(top[0:rows, :], leaky[0:rows, 0:n * H], AX_X, ALU.max).then_inc(top_done, 1)
                for q in range(len(last.sizes) - 2 if last else 0):
                    add_group(last, q)
                if blk:
                    dve.wait_ge(top_turned, blk.b + 1)
                    dve.tensor_scalar(turned_top[0:1, 0:rows], banks[5][0:1, 320:320 + rows], run_max[1 - s][0:1, 0:1], LOWEST,
                                      ALU.max, ALU.max, accum_out=run_max[s][0:1, 0:1]).then_inc(max_run, 1)
                if last and len(last.sizes) > 1:
                    add_group(last, len(last.sizes) - 2)
                if nxt:
                    hot16_rows(nxt)
                if blk:
                    dve.wait_ge(prob_ready, blk.b * 2 + 2)
                    for q, size in enumerate(blk.sizes):
                        c0 = q * GROUP
                        v = gathered(s, TW)[0:rows, c0:c0 + size, 0:D].rearrange("p c (h o) -> p c h o", h=H)
                        pr = gathered(s, TW)[0:rows, c0:c0 + size, D:D + H]
                        dve.tensor_tensor(v, v, pr.unsqueeze(3).broadcast_to((rows, size, H, HD)), ALU.mult).then_inc(scaled, 1)
                if last:
                    add_group(last, len(last.sizes) - 1)

            def attend_windows():
                hot16_rows(full_block(0, 0))
                over_blocks_ahead(dve, attend)

            def plain_scores(i, c, rows):
                chain, at = plain_chain, i * CHUNKS * 3
                sc, lk = score[0:rows, 0:H], leaky[0:rows, 0:H]
                dve.wait_ge(plain_rows, c * 32 + (i * CHUNKS + 1) * 32)
                dve.sem_inc(waited, 1)
                dve.tensor_reduce(lk, plain_adst[0:rows, :].rearrange("p (a h) -> p h a", a=PARTS), AX_X, ALU.add).then_inc(chain, 1)
                dve.wait_ge(chain, c * 3 + (at + 1))
                dve.sem_inc(waited, 1)
                dve.tensor_tensor(sc, gathered(0, TW)[0:rows, 0, D:D + H], lk, ALU.add).then_inc(chain, 1)
                dve.wait_ge(chain, c * 3 + (at + 2))
                dve.sem_inc(waited, 1)
                dve.scalar_tensor_tensor(out=lk, in0=sc, scalar=0.2, in1=sc, op0=ALU.mult, op1=ALU.max).then_inc(chain, 1)
                dve.wait_ge(chain, c * 3 + (at + 3))
                dve.sem_inc(waited, 1)

            def plain_peak(c, rows):
                plain_scores(0, c, rows)
                dve.tensor_tensor(peak[0:rows, :], peak[0:rows, :], leaky[0:rows, 0:H], ALU.max).then_inc(plain_peaked, 1)
                dve.wait_ge(plain_peaked, c + 1)
                dve.sem_inc(plain_free, 1)

            def plain_add(i, r):
                def step(c, rows):
                    if r == 0:
                        plain_scores(i, c, rows)
                        dve.sem_inc(plain_scored, 1)
                        dve.wait_ge(plain_weighed, c + 1)
                        dve.sem_inc(waited, 1)
                        v = gathered(0, TW)[0:rows, 0, 0:D].rearrange("p (h o) -> p h o", h=H)
                        dve.tensor_tensor(v, v, gathered(0, TW)[0:rows, 0, D:D + H].unsqueeze(2).broadcast_to((rows, H, HD)),
                                          ALU.mult).then_inc(plain_scaled, 1)
                    else:
                        dve.wait_ge(plain_rows, c * 16 + ((i + 2) * CHUNKS + 1) * 16)
                        v = gathered(0, widths[r])[0:rows, 0, :]
                        dve.tensor_tensor(v, v, w_now[0:rows, bass.ds(c, 1)].broadcast_to((rows, D)), ALU.mult).then_inc(plain_scaled, 1)
                    dve.wait_ge(plain_ids_in, c * 32 + (i * CHUNKS + 1) * 32)
                    dve.sem_inc(waited, 1)
                    dve.wait_ge(plain_turned, c + ((i - 1) * CHUNKS + 1))
                    dve.sem_inc(waited, 1)
                    turned = banks[6][:, 0:KB * P].rearrange("p (k e) -> p k e", k=KB)
                    with dve.Fori(0, rows) as e:
                        node = dve.value_load(plain_row[0:1, bass.ds(e, 1)], min_val=0, max_val=N - 1)
                        col = sums3[:, :, bass.ds(node, 1)]
                        add = dve.tensor_tensor(col, col, turned[:, :, bass.ds(e, 1)], ALU.add)
                        if r == 0:
                            col = heads[0:H, bass.ds(node, 1)]
                            add = dve.tensor_tensor(col, col, banks[7][0:H, bass.ds(e, 1)], ALU.add)
                        add.then_inc(plain_added, 1)
                        dve.wait_ge(plain_added, c * P + e + ((i - 1) * E + 1))
                        dve.sem_inc(waited, 1)
                    dve.sem_inc(plain_free, 1)

                def run():
                    dve.sem_inc(plain_free, 1)
                    over_chunks(dve, step)
                    dve.sem_inc(R[r]["added"], GROUPS)
                return run

            def attend_plain():
                dve.memset(peak[:, :], LOWEST).then_inc(soft, 1)
                dve.wait_ge(soft, 1)
                dve.sem_inc(plain_free, 1)
                over_chunks(dve, plain_peak)
                dve.tensor_reduce(top[:, :], peak[:, :], AX_X, ALU.max).then_inc(top_done, 1)
                dve.wait_ge(top_turned, 1)
                dve.tensor_scalar(turned_top[0:1, :], banks[5][0:1, 320:320 + P], run_max[1][0:1, 0:1], LOWEST,
                                  ALU.max, ALU.max, accum_out=run_max[0][0:1, 0:1]).then_inc(max_run, 1)
                dve.wait_ge(neg_ready, 2)
                plain_add(1, 0)()
            by_windows(dve, attend_windows, attend_plain)

            def moments(bt, y, chain, count, done):
                n, s = bt.rows, bt.slot
                for t in range(bt.tiles):
                    last = dve.bn_stats(stats_c[s][0:n, t, :], y[s][0:n, t, :])
                last.then_inc(chain, 1)
                dve.wait_ge(chain, count + 1)
                dve.sem_inc(waited, 1)
                for t in range(bt.tiles):
                    last = dve.bn_aggr(mv_c[s][0:n, t, :], stats_c[s][0:n, t, :])
                last.then_inc(done, 1)

            def shift(dev, rstd_sem, done):
                def step(bt):
                    n, s, t = bt.rows, bt.slot, bt.tiles
                    dve.wait_ge(dev, bt.b + 1)
                    dve.reciprocal(rstd_c[s][0:n, 0:t], dev_c[s][0:n, 0:t]).then_inc(rstd_sem, 1)
                    dve.wait_ge(rstd_sem, bt.b + 1)
                    dve.scalar_tensor_tensor(out=shift_c[s][0:n, 0:t], in0=mv_c[s][0:n, 0:t, 0], scalar=-1.0, in1=rstd_c[s][0:n, 0:t],
                                             op0=ALU.mult, op1=ALU.mult).then_inc(done, 1)
                return step

            def attention(bt):
                n, s, t = bt.rows, bt.slot, bt.tiles
                k = bt.b * 4
                hv = banks[4 + s][0:n, 0:t * (REC + 1)].rearrange("p (t r) -> p t r", t=t)
                rcp = rcp_c[s][0:n, 0:t * H].rearrange("p (t h) -> p t h", t=t)
                att = wide[s][0:n, 0:t * D].rearrange("p (a o) -> p a o", o=HD)
                dve.wait_ge(p1_turned, bt.b + 1)
                dve.tensor_copy(guard_c[s][0:n, 0:t], hv[:, :, REC]).then_inc(p1_chain, 1)
                dve.wait_ge(p1_chain, k + 1)
                dve.scalar_tensor_tensor(out=rcp, in0=guard_c[s][0:n, 0:t].unsqueeze(2).broadcast_to((n, t, H)), scalar=1e-10,
                                         in1=hv[:, :, 0:H], op0=ALU.mult, op1=ALU.add).then_inc(p1_chain, 1)
                dve.wait_ge(p1_chain, k + 2)
                dve.reciprocal(rcp, rcp).then_inc(p1_chain, 1)
                dve.wait_ge(p1_chain, k + 3)
                dve.tensor_tensor(att, att, rcp_c[s][0:n, 0:t * H].unsqueeze(2).broadcast_to((n, t * H, HD)), ALU.mult).then_inc(p1_att, 1)

            def residual(bt):
                n, s, t = bt.rows, bt.slot, bt.tiles
                at_least(dve, p1_out[s], 16 * bt.turn)
                dve.wait_ge(p1_x[s], 16 * (bt.turn + 1))
                dve.wait_ge(p1_att, bt.b + 1)
                dve.scalar_tensor_tensor(out=res1[s][0:n, 0:t, :], in0=x_res[s][0:n, 0:t, :], scalar=2.0,
                                         in1=wide[s][0:n, 0:t * D].rearrange("p (t f) -> p t f", t=t),
                                         op0=ALU.mult, op1=ALU.add).then_inc(p1_y, 1)
                dve.wait_ge(p1_y, bt.b + 1)
                moments(bt, res1, p1_chain, bt.b * 4 + 3, p1_var)
            shift1 = shift(p1_dev, p1_rstd, p1_shift)

            def finish1(bt):
                attention(bt)
                if bt.slot == 1:
                    shift1(bt._replace(b=bt.b - 1, slot=0, rows=P))
                residual(bt)
                if bt.slot == 1:
                    shift1(bt)
            over_batches(dve, T1, finish1)

            dve.wait_ge(p1_turned, batches(T1))
            dve.wait_ge(p1_copied, 2 * batches(T1))
            dve.wait_ge(root_x, 16)
            dve.scalar_tensor_tensor(out=root_cols[:, KB:2 * KB], in0=root_cols[:, 0:KB], scalar=0.01, in1=root_cols[:, 0:KB],
                                     op0=ALU.mult, op1=ALU.max).then_inc(root_step, 1)
            dve.wait_ge(root_step, 1)
            dve.tensor_copy(root_wide[:, :, :], root_cols[:, KB:2 * KB].unsqueeze(2).broadcast_to((P, KB, P))).then_inc(root_step, 1)
            dve.wait_ge(root_mm, 1)
            dve.tensor_copy(root1_row, banks[4][:, 0:D]).then_inc(root_ok, 1)
            dve.wait_ge(weights_in, 16 * 9)

            def weighted_hot(r, blk):
                n, rows, s = sum(blk.sizes), blk.rows, blk.slot
                at_least(dve, R[r]["added"], (blk.b - 1) * BLOCK_GROUPS)
                dve.sem_inc(waited, 1)
                one_hot(r, blk, hot[s], hot_step)
                dve.wait_ge(hot_step, (r - 1) * NBLOCKS + blk.b + 1)
                h3 = hot[s][0:rows, 0:n * WINDOW].rearrange("p (c j) -> p c j", j=WINDOW)
                dve.tensor_tensor(h3, h3, w_now[0:rows, bass.ds(blk.chunk, n)].unsqueeze(2).broadcast_to((rows, n, WINDOW)),
                                  ALU.mult).then_inc(R[r]["hot_ready"], 1)

            def add_weighted(r, blk, q):
                half = (blk.slot + q) % 2
                base = window_start(blk, q)
                dve.wait_ge(R[r]["group_turned"], blk.group + q + 1)
                at_least(dve, R[r]["added"], blk.group + q)
                win = sums3[:, :, bass.ds(base, WINDOW)]
                new = banks[6 + half][:, 0:KB * WINDOW].rearrange("p (k j) -> p k j", k=KB)
                dve.tensor_tensor(win, win, new, ALU.add).then_inc(R[r]["added"], 1)

            def leaky_h(ready, done):
                def step(bt):
                    s, n = bt.slot, bt.rows
                    dve.wait_ge(ready, 2 * bt.b + 2)
                    dve.scalar_tensor_tensor(out=h_t[s][:, :, 0:n], in0=h_t[s][:, :, 0:n], scalar=0.01, in1=h_t[s][:, :, 0:n],
                                             op0=ALU.mult, op1=ALU.max).then_inc(done, 1)
                return step

            def add_row(mm, out_sem, row, res, done):
                def step(bt):
                    n, s = bt.rows, bt.slot
                    dve.wait_ge(mm, bt.b + 1)
                    at_least(dve, out_sem[s], 16 * bt.turn)
                    dve.tensor_tensor(res[s][0:n, 0, :], banks[4 + s][0:n, 0:D], row[0:n, :], ALU.add).then_inc(done, 1)
                return step

            def dve_round(r, i, features, rows_step, shift_step):
                def step(blk, nxt, bt):
                    n = len(blk.sizes)
                    if nxt:
                        weighted_hot(r, nxt)
                    if bt:
                        features(bt)
                    add_weighted(r, blk, 0)
                    if bt:
                        rows_step(bt)
                    if n > 1:
                        add_weighted(r, blk, 1)
                    if bt and shift_step:
                        shift_step(bt)
                    if n > 2:
                        add_weighted(r, blk, 2)

                stages = [lambda blk, bt, stage=stage: stage(bt) for stage in (features, rows_step, shift_step) if stage]

                def clear():
                    dve.memset(sums[:, :], 0.0).then_inc(cleared, 1)
                    dve.wait_ge(cleared, r)

                def windows():
                    weighted_hot(r, full_block(0, 0))
                    clear()
                    over_blocks_batches(dve, step, *stages)

                def plain():
                    clear()
                    plain_add(i, r)()
                    over_node_batches(dve, *stages)
                by_windows(dve, windows, plain)

            dve.wait_ge(root_ok, 1)
            dve_round(1, 2, leaky_h(p2_act, p2_leaky), add_row(p2_z, p2_out, root1_row, row2, p2_row), None)

            dve.wait_ge(root2_mm, 1)
            dve.tensor_tensor(root_cols[:, 2 * KB:3 * KB], banks[7][:, 0:KB], bias_cols[:, 0:KB], ALU.add).then_inc(root2_step, 1)
            dve.wait_ge(root2_step, 1)
            dve.tensor_copy(root_wide[:, :, :], root_cols[:, 2 * KB:3 * KB].unsqueeze(2).broadcast_to((P, KB, P))).then_inc(root2_step, 1)
            dve.wait_ge(root2_mm, 2)
            dve.tensor_copy(root2_row, banks[6][:, 0:D]).then_inc(root2_ok, 1)

            dve.wait_ge(root2_ok, 1)
            dve.wait_ge(p2_h, 2 * TURNS)
            add_root2 = add_row(p3_mm, p3_out, root2_row, res3, p3_pre)

            def finish3(bt):
                n, s = bt.rows, bt.slot
                y = res3[s][0:n, 0, :]
                add_root2(bt)
                dve.wait_ge(p3_pre, bt.b + 1)
                dve.scalar_tensor_tensor(out=y, in0=y, scalar=0.01, in1=y, op0=ALU.mult, op1=ALU.max).then_inc(p3_leaky, 1)
                dve.wait_ge(p3_leaky, bt.b + 1)
                dve.wait_ge(p3_x[s], 16 * (bt.turn + 1))
                dve.tensor_tensor(y, y, x1_in[s][0:n, 0, :], ALU.add).then_inc(p3_y, 1)
                dve.wait_ge(p3_y, bt.b + 1)
                moments(bt, res3, p3_chain, bt.b, p3_var)
            dve_round(2, 3, leaky_h(p3_act, p3_in), finish3, shift(p3_dev, p3_rstd, p3_shift))


_INS = ["x", "src", "dst", "edge_weight", "L0_gnn_W", "L0_gnn_a_src", "L0_gnn_a_dst", "L1_gnn_W1", "L1_gnn_b1",
        "L1_gnn_W2", "L1_gnn_b2", "L1_gnn_Wl", "L1_gnn_bl", "L1_gnn_root_idx"]


def kernel(**inputs):
    import concourse.bacc as bacc
    from concourse.bass_utils import run_bass_kernel_spmd

    nc = bacc.Bacc("TRN2", target_bir_lowering=False, num_devices=1)
    arrays, args = {}, {}
    for name in _INS:
        v = np.ascontiguousarray(inputs[name])
        arrays[f"in_{name}"] = v
        args[name] = nc.dram_tensor(f"in_{name}", v.shape, mybir.dt.from_np(v.dtype), kind="ExternalInput").ap()
    out = nc.dram_tensor("out_0", arrays["in_x"].shape, F32, kind="ExternalOutput").ap()
    build(nc, args, out)
    result = run_bass_kernel_spmd(nc, [arrays], core_ids=[0])
    return result.results[0]["out_0"]
```
